# Optimizing a Trainium2 kernel written in Bass

```python
import numpy as np
import jax
import jax.numpy as jnp

def _softmax(x, axis=-1):
    return jax.nn.softmax(x, axis=axis)

def _gelu(x):
    return jax.nn.gelu(x, approximate=True)

def _silu(x):
    return jax.nn.silu(x)

def _sigmoid(x):
    return jax.nn.sigmoid(x)

def _layernorm(x, axis=-1, eps=1e-05):
    m = jnp.mean(x, axis=axis, keepdims=True)
    v = jnp.var(x, axis=axis, keepdims=True)
    return (x - m) / jnp.sqrt(v + eps)

def _scatter_add(tgt, idx, src, axis=0):
    return tgt.at[idx].add(src)

def _segment_sum(src, seg, n):
    return jax.ops.segment_sum(src, seg, n)
kernel_name = 'mk_audio_tower_d1_tok_audfeat512_r4_9cf363'

def setup_inputs(seed: int=0):
    np.random.seed(seed)
    _w = jnp.asarray

    def _rec_inputs():
        import jax
        import jax.numpy as jnp
        _rk = jax.random.key(seed)
        x = -0.000292821 + 1.00034 * jax.random.normal(jax.random.fold_in(_rk, 1), (64, 750, 2), jnp.float32)
        return x
    x = _rec_inputs()

    def _L0_tok_setup():
        import jax, jax.numpy as jnp
        import numpy as np
        PATCH_LENGTH = 128
        PATCH_STRIDE = 64
        MODEL_DIM = 128
        LN_EPS = 0.001
        key = jax.random.key(seed)
        k1, k2 = jax.random.split(key)
        B, T, C = (64, 8192, 2)
        x = jax.random.normal(k1, (B, T, C), dtype=jnp.float32)
        in_dim = PATCH_LENGTH * C
        W = jax.random.normal(k2, (in_dim, MODEL_DIM), dtype=jnp.float32) / np.sqrt(in_dim)
        b = jnp.zeros((MODEL_DIM,), dtype=jnp.float32)
        gamma = jnp.ones((MODEL_DIM,), dtype=jnp.float32)
        beta = jnp.zeros((MODEL_DIM,), dtype=jnp.float32)
        return {'x': x, 'W': W, 'b': b, 'gamma': gamma, 'beta': beta}
    _L0_tok_all = _L0_tok_setup()
    _L0_tok_in = {k: v for k, v in _L0_tok_all.items() if k in ('W', 'b', 'gamma', 'beta')}
    del _L0_tok_all

    def _L0_attn_setup():
        import jax, jax.numpy as jnp
        import numpy as np
        B, S, E, H = (2, 1024, 128, 8)
        D = E // H
        key = jax.random.key(seed)
        ks = jax.random.split(key, 6)
        x = jax.random.normal(ks[0], (B, S, E), dtype=jnp.float32)
        scale = E ** (-0.5)
        in_proj_w = jax.random.normal(ks[1], (3 * E, E), dtype=jnp.float32) * scale
        in_proj_b = jnp.zeros((3 * E,), dtype=jnp.float32)
        out_proj_w = jax.random.normal(ks[2], (E, E), dtype=jnp.float32) * scale
        out_proj_b = jnp.zeros((E,), dtype=jnp.float32)
        t = jax.random.normal(ks[3], (H,), dtype=jnp.float32)
        return {'x': x, 'in_proj_w': in_proj_w, 'in_proj_b': in_proj_b, 'out_proj_w': out_proj_w, 'out_proj_b': out_proj_b, 't': t}
    _L0_attn_all = _L0_attn_setup()
    _L0_attn_in = {k: v for k, v in _L0_attn_all.items() if k in ('in_proj_w', 'in_proj_b', 'out_proj_w', 'out_proj_b', 't')}
    del _L0_attn_all

    def _L0_ffn_setup():
        import jax, jax.numpy as jnp
        import numpy as np
        B, S, H, E, F, TOP_K = (4, 512, 128, 16, 256, 2)

        def _moe_forward(inputs, router_w, gate_w, up_w, down_w):
            b, s, h = inputs.shape
            x = inputs.reshape(-1, h)
            T = x.shape[0]
            router_logits = x @ router_w.T
            top_vals, top_idx = jax.lax.top_k(router_logits, TOP_K)
            weights = jax.nn.softmax(top_vals.astype(jnp.float32), axis=-1)
            combine = jnp.zeros((T, router_w.shape[0]), jnp.float32)
            combine = combine.at[jnp.arange(T)[:, None], top_idx].set(weights)

            def step(acc, ew):
                wg, wu, wd, ce = ew
                hid = jax.nn.silu(x @ wg) * (x @ wu)
                y = hid @ wd
                return (acc + ce[:, None] * y, None)
            out0 = jnp.zeros_like(x)
            out, _ = jax.lax.scan(step, out0, (gate_w, up_w, down_w, combine.T))
            return (out.reshape(b, s, h), router_logits, top_idx)
        key = jax.random.key(seed)
        k0, k1, k2, k3, k4 = jax.random.split(key, 5)
        scale = 0.02
        return {'inputs': jax.random.normal(k0, (B, S, H), dtype=jnp.float32), 'router_w': jax.random.normal(k1, (E, H), dtype=jnp.float32) * scale, 'gate_w': jax.random.normal(k2, (E, H, F), dtype=jnp.float32) * scale, 'up_w': jax.random.normal(k3, (E, H, F), dtype=jnp.float32) * scale, 'down_w': jax.random.normal(k4, (E, F, H), dtype=jnp.float32) * scale}
    _L0_ffn_all = _L0_ffn_setup()
    _L0_ffn_in = {k: v for k, v in _L0_ffn_all.items() if k in ('router_w', 'gate_w', 'up_w', 'down_w')}
    del _L0_ffn_all
    return {'x': x, 'L0_tok_W': _L0_tok_in['W'], 'L0_tok_b': _L0_tok_in['b'], 'L0_tok_gamma': _L0_tok_in['gamma'], 'L0_tok_beta': _L0_tok_in['beta'], 'L0_attn_in_proj_w': _L0_attn_in['in_proj_w'], 'L0_attn_in_proj_b': _L0_attn_in['in_proj_b'], 'L0_attn_out_proj_w': _L0_attn_in['out_proj_w'], 'L0_attn_out_proj_b': _L0_attn_in['out_proj_b'], 'L0_attn_t': _L0_attn_in['t'], 'L0_ffn_router_w': _L0_ffn_in['router_w'], 'L0_ffn_gate_w': _L0_ffn_in['gate_w'], 'L0_ffn_up_w': _L0_ffn_in['up_w'], 'L0_ffn_down_w': _L0_ffn_in['down_w']}

def reference(x, L0_tok_W, L0_tok_b, L0_tok_gamma, L0_tok_beta, L0_attn_in_proj_w, L0_attn_in_proj_b, L0_attn_out_proj_w, L0_attn_out_proj_b, L0_attn_t, L0_ffn_router_w, L0_ffn_gate_w, L0_ffn_up_w, L0_ffn_down_w):
    import jax
    import jax.numpy as jnp

    def _L0_tok_ref(x, W, b, gamma, beta):
        import jax, jax.numpy as jnp
        import numpy as np
        PATCH_LENGTH = 128
        PATCH_STRIDE = 64
        MODEL_DIM = 128
        LN_EPS = 0.001
        B, T, C = x.shape
        num_patches = (T - PATCH_LENGTH) // PATCH_STRIDE + 1
        idx = jnp.arange(num_patches)[:, None] * PATCH_STRIDE + jnp.arange(PATCH_LENGTH)[None, :]
        patches = x[:, idx, :]
        patches = patches.reshape(B, num_patches, PATCH_LENGTH * C)
        proj = jnp.einsum('bpf,fd->bpd', patches, W) + b
        mean = jnp.mean(proj, axis=-1, keepdims=True)
        var = jnp.mean(jnp.square(proj - mean), axis=-1, keepdims=True)
        out = (proj - mean) * jax.lax.rsqrt(var + LN_EPS) * gamma + beta
        return out

    def _L0_attn_ref(x, in_proj_w, in_proj_b, out_proj_w, out_proj_b, t):
        import jax, jax.numpy as jnp
        import numpy as np
        B, S, E, H = (2, 1024, 128, 8)
        D = E // H
        b, s, e = x.shape
        h, d = (H, D)
        qkv = x @ in_proj_w.T + in_proj_b
        q, k, v = jnp.split(qkv, 3, axis=-1)
        q = q.reshape(b, s, h, d).transpose(0, 2, 1, 3)
        k = k.reshape(b, s, h, d).transpose(0, 2, 1, 3)
        v = v.reshape(b, s, h, d).transpose(0, 2, 1, 3)
        scores = jnp.einsum('bhqd,bhkd->bhqk', q, k) / jnp.sqrt(jnp.float32(d))
        idx = jnp.arange(s)
        dist2 = (idx[None, :] - idx[:, None]).astype(jnp.float32) ** 2
        sigma = t ** 2
        bias = -dist2[None, :, :] / (2.0 * (sigma ** 2)[:, None, None])
        attn = jax.nn.softmax(scores + bias[None], axis=-1)
        out = jnp.einsum('bhqk,bhkd->bhqd', attn, v)
        out = out.transpose(0, 2, 1, 3).reshape(b, s, e)
        return out @ out_proj_w.T + out_proj_b

    def _L0_ffn_ref(inputs, router_w, gate_w, up_w, down_w):
        import jax, jax.numpy as jnp
        import numpy as np
        B, S, H, E, F, TOP_K = (4, 512, 128, 16, 256, 2)

        def _moe_forward(inputs, router_w, gate_w, up_w, down_w):
            b, s, h = inputs.shape
            x = inputs.reshape(-1, h)
            T = x.shape[0]
            router_logits = x @ router_w.T
            top_vals, top_idx = jax.lax.top_k(router_logits, TOP_K)
            weights = jax.nn.softmax(top_vals.astype(jnp.float32), axis=-1)
            combine = jnp.zeros((T, router_w.shape[0]), jnp.float32)
            combine = combine.at[jnp.arange(T)[:, None], top_idx].set(weights)

            def step(acc, ew):
                wg, wu, wd, ce = ew
                hid = jax.nn.silu(x @ wg) * (x @ wu)
                y = hid @ wd
                return (acc + ce[:, None] * y, None)
            out0 = jnp.zeros_like(x)
            out, _ = jax.lax.scan(step, out0, (gate_w, up_w, down_w, combine.T))
            return (out.reshape(b, s, h), router_logits, top_idx)
        out, router_logits, selected_experts = _moe_forward(inputs, router_w, gate_w, up_w, down_w)
        return out
    h = _L0_tok_ref(x, L0_tok_W, L0_tok_b, L0_tok_gamma, L0_tok_beta)
    h = h + _L0_attn_ref(_layernorm(h, axis=-1), L0_attn_in_proj_w, L0_attn_in_proj_b, L0_attn_out_proj_w, L0_attn_out_proj_b, L0_attn_t)
    h = h + _L0_ffn_ref(_layernorm(h, axis=-1), L0_ffn_router_w, L0_ffn_gate_w, L0_ffn_up_w, L0_ffn_down_w)
    return h

_drawn_inputs = setup_inputs


def setup_inputs(seed=0):
    import zlib

    import numpy as np

    out = dict(_drawn_inputs(seed))
    spreads = {'L0_tok_b': (0.0, 0.1),
     'L0_tok_gamma': (1.0, 0.2),
     'L0_tok_beta': (0.0, 0.1),
     'L0_attn_in_proj_b': (0.0, 0.1),
     'L0_attn_out_proj_b': (0.0, 0.1)}
    factors = {'L0_ffn_router_w': 8.0, 'L0_ffn_gate_w': 8.0, 'L0_ffn_up_w': 8.0, 'L0_ffn_down_w': 8.0}
    for name, (base, spread) in spreads.items():
        noise = np.random.default_rng([zlib.crc32(name.encode()), seed]).standard_normal(out[name].shape)
        drawn = base * np.exp(spread * noise) if base else spread * noise
        out[name] = jnp.asarray(drawn.astype(out[name].dtype))
    for name, factor in factors.items():
        out[name] = (out[name] * factor).astype(out[name].dtype)
    return out
```

```python
from contextlib import ExitStack

import numpy as np

import concourse.bass as bass
from concourse import mybir

F32 = mybir.dt.float32
U32 = mybir.dt.uint32
I32 = mybir.dt.int32
ALU = mybir.AluOpType
ACT = mybir.ActivationFunctionType
AX_X = mybir.AxisListType.X

P = 128
B = 64
S = 10
T = S // 2
D = 128
H = 8
DH = D // H
E = 16
F = 256
TOPK = 2
TOK = B * S
CHUNKS = S + 1
WROW = 2 * F + F
MAXB = TOK // P
NOV = (TOK * TOPK - E) // P
ROWS = (E + NOV) * P
ROW = D + 2
NBUF = 4
EPS_TOK = 1e-3
EPS_LN = 1e-5
FAR = -1e30

C_ID = 0
C_TRI = C_ID + P
C_ONE = C_TRI + P
C_HEAD = C_ONE + P
C_IOTA = C_HEAD + H
C_EBASE = C_IOTA + E
C_PAR = C_EBASE + E
C_DIST = C_PAR + P
C_HALF = C_DIST + T * S
C_THR = C_HALF + T
C_BLK = C_THR + MAXB - 1
C_DST = C_BLK + NOV
C_END = C_DST + TOPK * T


def constants():
    p = np.arange(P)
    c = np.zeros((P, C_END), np.float32)
    c[:, C_ID:C_ID + P] = np.eye(P)
    c[:, C_TRI:C_TRI + P] = p[:, None] < p[None, :]
    c[:, C_ONE:C_ONE + P] = 1.0
    c[:, C_HEAD:C_HEAD + H] = (p[:, None] // DH == np.arange(H)[None, :]) * DH ** -0.5
    c[:, C_IOTA:C_IOTA + E] = np.arange(E)
    c[:, C_EBASE:C_EBASE + E] = np.arange(E) * P
    c[0:2, C_PAR:C_PAR + P] = np.arange(2)[:, None] == p[None, :] // B
    q = 2 * np.arange(T)[None, :, None] + np.arange(2)[:, None, None]
    c[0:2, C_DIST:C_DIST + T * S] = (-(q - np.arange(S)[None, None, :]) ** 2.0).reshape(2, T * S)
    c[:, C_HALF:C_HALF + T] = -0.5
    c[:, C_THR:C_THR + MAXB - 1] = P * np.arange(1, MAXB)
    c[:, C_BLK:C_BLK + NOV] = np.arange(NOV)
    dst = TOK * np.arange(TOPK)[:, None] + P * np.arange(T)[None, :]
    c[:, C_DST:C_END] = dst.reshape(1, -1) + p[:, None]
    return c


def audio_tower(nc, x_t, tok_w, tok_b, gamma, beta, qkv_wt, qk_b, v_b, out_wt, out_b, t_head,
                router_wt, expert_w, table, out):
    with ExitStack() as ctx:
        def sb(name, shape, dt=F32):
            return ctx.enter_context(nc.sbuf_tensor(name, shape, dt))

        def sem(name):
            return ctx.enter_context(nc.semaphore(name))

        ps = ctx.enter_context(nc.psum_tensor("ps", [P, 8, 512], F32))

        xT = sb("xT", [P, CHUNKS * B])
        tokW = sb("tokW", [P, 2, D])
        rows = sb("rows", [1, 3, D])
        gam = sb("gam", [P, D])
        bet = sb("bet", [P, D])
        qkvW = sb("qkvW", [P, 3 * D])
        qkB = sb("qkB", [P, 2])
        outW = sb("outW", [P, D])
        routeW = sb("routeW", [P, E])
        headT = sb("headT", [2, H])
        cst = sb("cst", [P, C_END])
        expW = sb("expW", [P, E * WROW])

        stats = sb("stats", [P, T, 6])
        mv = sb("mv", [P, T, 2])
        mve = sb("mve", [P, T])
        rstd = sb("rstd", [P, T])
        h = sb("h", [P, T, D])
        xn = sb("xn", [P, T, D])
        xnT = sb("xnT", [P, S, 2, B])
        qT = sb("qT", [P, TOK])
        kT = sb("kT", [P, TOK])
        sig = sb("sig", [2, 4, H])
        bias = sb("bias", [2, T, S * H])
        prod = sb("prod", [P, 2, S * P])
        mx = sb("mx", [P, 2, H])
        sc = sb("sc", [P, 2, S * H])
        ex = sb("ex", [P, 2, S * H])
        den = sb("den", [P, 2, H])
        rden = sb("rden", [P, 2, H])
        pn = sb("pn", [P, 2, S * H])
        prodv = sb("prodv", [P, 2, S * D])
        oT = sb("oT", [P, T, P])
        h2 = sb("h2", [P, T, D])
        pay = sb("pay", [P, TOPK, T, ROW])
        x2T = sb("x2T", [P, T, P])
        lg = sb("lg", [P, T, E])
        top = sb("top", [P, T, 8])
        topi = sb("topi", [P, T, 8], U32)
        idxf = sb("idxf", [P, T, TOPK])
        oh = sb("oh", [P, T, TOPK, E])
        mask = sb("mask", [P, T, E])
        dlt = sb("dlt", [P, T])
        ed = sb("ed", [P, T])
        ed1 = sb("ed1", [P, T])
        ovm = sb("ovm", [P, E, MAXB - 1])
        nov = sb("nov", [P, E])
        novi = sb("novi", [P, E])
        dif = sb("dif", [P, E])
        dif2 = sb("dif2", [P, E])
        s1 = sb("s1", [P, T, E])
        s2 = sb("s2", [P, T, E])
        s3 = sb("s3", [P, T, E])
        s4 = sb("s4", [P, T, TOPK, E])
        slotf = sb("slotf", [P, T * TOPK])
        slot = sb("slot", [P, T * TOPK], U32)
        eom = sb("eom", [1, NOV, E])
        eof = sb("eof", [1, NOV])
        ctl = sb("ctl", [1, 1 + NOV], I32)
        blank = sb("blank", [P, ROW])
        xs = sb("xs", [P, NBUF, ROW])
        xsT = sb("xsT", [P, 2, P])
        sg = sb("sg", [P, 2, F])
        hid = sb("hid", [P, 2, F])
        hidT = sb("hidT", [P, 2, 2, P])
        ys = sb("ys", [P, NBUF, D])
        yi = sb("yi", [P, NBUF], U32)
        yb = sb("yb", [P, TOPK, T, D])
        acc = sb("acc", [P, T, D])
        fin = sb("fin", [P, T, D])

        disp = nc.dram_tensor("disp", [ROWS, ROW], F32).ap()
        ybuf = nc.dram_tensor("ybuf", [TOPK * TOK, D], F32).ap()

        in_first = sem("in_first")
        in_small = sem("in_small")
        in_expert = sem("in_expert")
        s_blank = sem("s_blank")
        s_filled = sem("s_filled")
        dv = sem("dv")
        var1 = sem("var1")
        rs = sem("rs")
        proj_ready = sem("proj_ready")
        xn_ready = sem("xn_ready")
        xnT_ps = sem("xnT_ps")
        xnT_ready = sem("xnT_ready")
        qk_ps = sem("qk_ps")
        qk_ready = sem("qk_ready")
        v_ps = sem("v_ps")
        bias_ready = sem("bias_ready")
        prod_ready = sem("prod_ready")
        scores_ps = sem("scores_ps")
        sub_ready = sem("sub_ready")
        exp_ready = sem("exp_ready")
        pv_ready = sem("pv_ready")
        o_ps = sem("o_ps")
        oT_ready = sem("oT_ready")
        a_ps = sem("a_ps")
        x2_ready = sem("x2_ready")
        pay_ready = sem("pay_ready")
        x2T_ps = sem("x2T_ps")
        x2T_ready = sem("x2T_ready")
        lg_ps = sem("lg_ps")
        lg_ready = sem("lg_ready")
        dlt_ready = sem("dlt_ready")
        ed_ready = sem("ed_ready")
        mask_ready = sem("mask_ready")
        rank_ps = sem("rank_ps")
        slot_ready = sem("slot_ready")
        ctl_ready = sem("ctl_ready")
        s_disp = sem("s_disp")
        xs_in = [sem(f"xs_in{u}") for u in range(NBUF)]
        xsT_ps = sem("xsT_ps")
        xsT_ready = sem("xsT_ready")
        g_ps = sem("g_ps")
        sg_ready = sem("sg_ready")
        hid_ready = sem("hid_ready")
        hidT_ps = sem("hidT_ps")
        hidT_ready = sem("hidT_ready")
        y_ps = sem("y_ps")
        y_ready = sem("y_ready")
        y_out = [sem(f"y_out{u}") for u in range(NBUF)]
        y_over = sem("y_over")
        over_done = sem("over_done")
        y_taken = sem("y_taken")
        yb_in = sem("yb_in")
        fin_ready = sem("fin_ready")
        s_out = sem("s_out")

        ident = cst[:, C_ID:C_ID + P]
        ones_row = cst[0:1, C_ONE:C_ONE + P]
        N_SMALL = 11

        def attn_out(t):
            return ps[:, 3, t * D:(t + 1) * D] if t < 4 else ps[:, 0, 0:D]

        X2_BANK = [5, 6, 7, 1, 2]

        block = ctx.enter_context(nc.Block())

        @block.sync
        def _(sp):
            sp.dma_start(xT[:, :], x_t).then_inc(in_first, 16)
            sp.dma_start(tokW[:, :, :], tok_w).then_inc(in_first, 16)
            sp.dma_start(rows[:, 0, :], tok_b).then_inc(in_small, 16)
            sp.dma_start(rows[:, 1, :], v_b).then_inc(in_small, 16)
            sp.dma_start(rows[:, 2, :], out_b).then_inc(in_small, 16)
            sp.dma_start(qkvW[:, :], qkv_wt).then_inc(in_small, 16)
            sp.dma_start(outW[:, :], out_wt).then_inc(in_small, 16)
            for g in range(0, E, NBUF):
                sp.dma_start(expW[:, g * WROW:(g + NBUF) * WROW],
                             expert_w[:, g * WROW:(g + NBUF) * WROW]).then_inc(in_expert, 16)
                if g == 0:
                    sp.wait_ge(s_blank, 2)
                    sp.dma_start(disp.rearrange("(n p) c -> p n c", p=P),
                                 blank[:, :].unsqueeze(1).broadcast_to([P, ROWS // P, ROW])
                                 ).then_inc(s_filled, 16)

            sp.wait_ge(s_disp, 16 * T * TOPK)
            for u in range(NBUF):
                sp.dma_start(xs[:, u, :], disp[u * P:(u + 1) * P, :]).then_inc(xs_in[u], 16)
            with sp.Fori(NBUF, E, NBUF) as e0:
                for u in range(NBUF):
                    row = sp.snap((e0 + u) * P)
                    sp.wait_ge(y_ready, e0 + (u - NBUF + 1))
                    sp.dma_start(xs[:, u, :], disp[bass.ds(row, P), :]).then_inc(xs_in[u], 16)
            sp.wait_ge(ctl_ready, 1)
            n_over = sp.value_load(ctl[0:1, 0:1], min_val=0, max_val=NOV)
            with sp.Fori(0, NOV) as i:
                with sp.If(i < n_over):
                    row = sp.snap((i + E) * P)
                    sp.wait_ge(y_ready, i + E)
                    sp.dma_start(xs[:, 0, :], disp[bass.ds(row, P), :]).then_inc(xs_in[0], 16)
                    sp.wait_ge(y_over, i * 16 + 16)
                    sp.sem_inc(over_done, 1)

            for u in range(NBUF):
                sp.wait_ge(y_out[u], 16 * (E // NBUF))
            yv = ybuf.rearrange("(j t p) c -> p (j t) c", j=TOPK, p=P)
            ysb = yb[:, :, :, :].rearrange("p j t c -> p (j t) c")
            sp.dma_start(ysb, yv).then_inc(yb_in, 16)
            ov = out.rearrange("b (t r) d -> r b t d", r=2)
            sp.wait_ge(fin_ready, 1)
            for r in range(2):
                sp.dma_start(ov[r], fin[r * B:(r + 1) * B, :, :]).then_inc(s_out, 16)
            sp.wait_ge(s_out, 32)

        @block.gpsimd
        def _(pool):
            nc.gpsimd.memset(blank[:, :], 0.0).then_inc(s_blank, 1)
            pool.wait_ge(s_blank, 1)
            nc.gpsimd.memset(blank[:, D:D + 1], float(4 * TOPK * TOK)).then_inc(s_blank, 1)
            pool.wait_ge(in_small, 16 * N_SMALL)
            for n in range(3):
                pool.wait_ge(var1, n + 1)
                nc.gpsimd.tensor_tensor(rstd[:, :], mve[:, :], cst[:, C_HALF:C_HALF + T],
                                        ALU.pow).then_inc(rs, 1)
            pool.wait_ge(s_filled, 16)
            pool.wait_ge(slot_ready, 1)
            for t in range(T):
                for j in range(TOPK):
                    if j == 1:
                        pool.wait_ge(pay_ready, t + 1)
                    n = t * TOPK + j
                    nc.gpsimd.indirect_dma_start(
                        out=disp, out_offset=bass.IndirectOffsetOnAxis(ap=slot[:, n:n + 1], axis=0),
                        in_=pay[:, j, t, :], in_offset=None).then_inc(s_disp, 16)

            def scatter(u, done):
                nc.gpsimd.indirect_dma_start(
                    out=ybuf, out_offset=bass.IndirectOffsetOnAxis(ap=yi[:, u:u + 1], axis=0),
                    in_=ys[:, u, :], in_offset=None, bounds_check=TOPK * TOK - 1,
                    oob_is_err=False).then_inc(done, 16)

            with pool.Fori(0, E, NBUF) as e0:
                for u in range(NBUF):
                    pool.wait_ge(y_ready, e0 + (u + 1))
                    pool.sem_inc(y_taken, 1)
                    scatter(u, y_out[u])
            n_over = pool.value_load(ctl[0:1, 0:1], min_val=0, max_val=NOV)
            with pool.Fori(0, NOV) as i:
                with pool.If(i < n_over):
                    pool.wait_ge(y_ready, i + (E + 1))
                    pool.sem_inc(y_taken, 1)
                    scatter(0, y_over)

        @block.scalar
        def _(act):
            act.dma_start(cst[:, :], table).then_inc(in_small, 16)
            act.dma_start(gam[:, :], gamma.partition_broadcast(P)).then_inc(in_small, 16)
            act.dma_start(bet[:, :], beta.partition_broadcast(P)).then_inc(in_small, 16)
            act.dma_start(qkB[:, :], qk_b).then_inc(in_small, 16)
            act.dma_start(headT[:, :], t_head.partition_broadcast(2)).then_inc(in_small, 16)
            act.dma_start(routeW[:, :], router_wt).then_inc(in_small, 16)
            act.wait_ge(in_small, 16 * N_SMALL)
            for t in range(T):
                act.wait_ge(xnT_ps, t + 1)
                nc.scalar.activation(xnT[:, 2 * t:2 * t + 2, :, :],
                                     ps[:, t, P:2 * P].rearrange("p (r b) -> p r b", r=2).unsqueeze(2)
                                     .broadcast_to([P, 2, 2, B]), ACT.Copy).then_inc(xnT_ready, 1)
            for n, dst in enumerate((qT, kT)):
                act.wait_ge(qk_ps, n + 1)
                nc.scalar.activation(dst[:, :], ps[:, 2 * n:2 * n + 2, :].rearrange("p a b -> p (a b)")[:, 0:TOK],
                                     ACT.Identity, bias=qkB[:, n:n + 1]).then_inc(qk_ready, 1)

            def exp(i):
                act.wait_ge(sub_ready, i + 1)
                nc.scalar.activation(ex[:, i % 2, :], sc[:, i % 2, :], ACT.Exp).then_inc(exp_ready, 1)

            def evac_o(i):
                act.wait_ge(o_ps, i + 1)
                nc.scalar.activation(oT[:, i, :], ps[:, 1 + i % 2, 0:P],
                                     ACT.Copy).then_inc(oT_ready, 1)

            for i in range(T + 2):
                if i < T:
                    exp(i)
                if i >= 2:
                    evac_o(i - 2)
            for t in range(T):
                act.wait_ge(x2_ready, t + 1)
                nc.scalar.activation(pay[:, 1, t, 0:D], pay[:, 0, t, 0:D], ACT.Copy).then_inc(pay_ready, 1)
                act.wait_ge(x2T_ps, t + 1)
                nc.scalar.activation(x2T[:, t, :], ps[:, X2_BANK[t], 0:P],
                                     ACT.Copy).then_inc(x2T_ready, 1)
            act.wait_ge(lg_ps, 1)
            nc.scalar.activation(lg[:, :, :].rearrange("p t e -> p (t e)"), ps[:, 4, 0:T * E],
                                 ACT.Copy).then_inc(lg_ready, 1)
            act.wait_ge(dlt_ready, 1)
            nc.scalar.activation(ed[:, :], dlt[:, :], ACT.Exp).then_inc(ed_ready, 1)

            def step(b, e):
                act.wait_ge(xsT_ps, e + 1)
                nc.scalar.activation(xsT[:, b, :], ps[:, 2, 0:P], ACT.Copy).then_inc(xsT_ready, 1)
                act.wait_ge(g_ps, e + 1)
                nc.scalar.activation(sg[:, b, :], ps[:, b, 0:F], ACT.Silu).then_inc(sg_ready, 1)

            with act.Fori(0, E, NBUF) as e0:
                for u in range(NBUF):
                    step(u % 2, e0 + u)
            act.wait_ge(ctl_ready, 1)
            n_over = act.value_load(ctl[0:1, 0:1], min_val=0, max_val=NOV)
            with act.Fori(0, NOV) as i:
                with act.If(i < n_over):
                    step(0, i + E)

        @block.vector
        def _(dve):
            count = [0]

            def mark(ins):
                count[0] += 1
                ins.then_inc(dv, 1)

            def settle():
                dve.wait_ge(dv, count[0])

            nc.vector.memset(ctl[:, :], 0).then_inc(hid_ready, 1)
            dve.wait_ge(in_small, 16 * N_SMALL)
            mark(nc.vector.tensor_tensor(sig[:, 0, :], headT[:, :], headT[:, :], ALU.mult))
            settle()
            mark(nc.vector.scalar_tensor_tensor(sig[:, 1, :], sig[:, 0, :], 2.0, sig[:, 0, :], ALU.mult, ALU.mult))
            settle()
            mark(nc.vector.tensor_scalar(sig[:, 2, :], sig[:, 1, :], 1e-37, None, ALU.max))
            settle()
            mark(nc.vector.reciprocal(sig[:, 3, :], sig[:, 2, :]))
            settle()
            mark(nc.vector.tensor_tensor(
                bias[:, :, :].rearrange("r t (k h) -> r (t k) h", h=H),
                cst[0:2, C_DIST:C_DIST + T * S].unsqueeze(2).broadcast_to([2, T * S, H]),
                sig[:, 3, :].unsqueeze(1).broadcast_to([2, T * S, H]), ALU.mult))
            settle()
            nc.vector.tensor_scalar(bias[:, :, :], bias[:, :, :], FAR, None, ALU.max).then_inc(bias_ready, 1)

            def variances(src, n):
                for t in range(T):
                    if n == 0:
                        dve.wait_ge(proj_ready, t + 1)
                    mark(nc.vector.bn_stats(stats[:, t, :], src(t)))
                settle()
                for t in range(T):
                    mark(nc.vector.bn_aggr(mv[:, t, :], stats[:, t, :]))
                settle()
                nc.vector.tensor_scalar(mve[:, :], mv[:, :, 1], EPS_TOK if n == 0 else EPS_LN, None,
                                        ALU.add).then_inc(var1, 1)
                dve.wait_ge(rs, n + 1)

            variances(lambda t: ps[:, t, 0:D], 0)
            for t in range(T):
                mark(nc.vector.tensor_scalar(h[:, t, :], ps[:, t, 0:D], mv[:, t, 0:1], rstd[:, t:t + 1],
                                             ALU.subtract, ALU.mult))
            settle()
            mark(nc.vector.tensor_tensor(h[:, :, :], h[:, :, :],
                                         gam[:, :].unsqueeze(1).broadcast_to([P, T, D]), ALU.mult))
            settle()
            mark(nc.vector.tensor_tensor(h[:, :, :], h[:, :, :],
                                         bet[:, :].unsqueeze(1).broadcast_to([P, T, D]), ALU.add))
            settle()
            variances(lambda t: h[:, t, :], 1)
            for t in range(T):
                nc.vector.tensor_scalar(xn[:, t, :], h[:, t, :], mv[:, t, 0:1], rstd[:, t:t + 1],
                                        ALU.subtract, ALU.mult).then_inc(xn_ready, 1)

            v4 = ps[:, 5:8, :].rearrange("p a b -> p (a b)")[:, 0:S * D]

            def products(i):
                if i >= 2:
                    dve.wait_ge(scores_ps, i - 1)
                nc.vector.tensor_tensor(
                    prod[:, i % 2, :].rearrange("p (k r b) -> p k r b", k=S, r=2),
                    qT[:, i * P:(i + 1) * P].rearrange("p (r b) -> p r b", r=2).unsqueeze(1)
                    .broadcast_to([P, S, 2, B]),
                    kT[:, :].rearrange("p (k b) -> p k b", k=S).unsqueeze(2).broadcast_to([P, S, 2, B]),
                    ALU.mult).then_inc(prod_ready, 1)

            def minus_max(i):
                b = i % 2
                dve.wait_ge(scores_ps, i + 1)
                s = ps[:, 4 * (1 - b), 0:S * H]
                mark(nc.vector.tensor_reduce(mx[:, b, :], s.rearrange("p (k h) -> p h k", h=H), AX_X, ALU.max))
                settle()
                nc.vector.tensor_tensor(
                    sc[:, b, :].rearrange("p (k h) -> p k h", h=H), s.rearrange("p (k h) -> p k h", h=H),
                    mx[:, b, :].unsqueeze(1).broadcast_to([P, S, H]), ALU.subtract).then_inc(sub_ready, 1)

            def weighted_values(i):
                b = i % 2
                dve.wait_ge(exp_ready, i + 1)
                mark(nc.vector.tensor_reduce(den[:, b, :], ex[:, b, :].rearrange("p (k h) -> p h k", h=H),
                                             AX_X, ALU.add))
                settle()
                mark(nc.vector.reciprocal(rden[:, b, :], den[:, b, :]))
                settle()
                mark(nc.vector.tensor_tensor(
                    pn[:, b, :].rearrange("p (k h) -> p k h", h=H),
                    ex[:, b, :].rearrange("p (k h) -> p k h", h=H),
                    rden[:, b, :].unsqueeze(1).broadcast_to([P, S, H]), ALU.mult))
                settle()
                if i == 0:
                    dve.wait_ge(v_ps, 1)
                if i >= 2:
                    dve.wait_ge(o_ps, i - 1)
                nc.vector.tensor_tensor(
                    prodv[:, b, :].rearrange("p (n d) -> p n d", d=DH),
                    v4.rearrange("p (n d) -> p n d", d=DH),
                    pn[:, b, :].unsqueeze(2).broadcast_to([P, S * H, DH]), ALU.mult).then_inc(pv_ready, 1)

            dve.wait_ge(qk_ready, 2)
            for i in range(T + 2):
                if i < T:
                    products(i)
                if 1 <= i <= T:
                    minus_max(i - 1)
                if i >= 2:
                    weighted_values(i - 2)
            for t in range(T):
                dve.wait_ge(a_ps, T)
                mark(nc.vector.tensor_tensor(h2[:, t, :], attn_out(t), h[:, t, :], ALU.add))
            settle()
            variances(lambda t: h2[:, t, :], 2)
            for t in range(T):
                nc.vector.tensor_scalar(pay[:, 0, t, 0:D], h2[:, t, :], mv[:, t, 0:1], rstd[:, t:t + 1],
                                        ALU.subtract, ALU.mult).then_inc(x2_ready, 1)
            nc.vector.tensor_copy(pay[:, :, :, D], cst[:, C_DST:C_END].rearrange("p (j t) -> p j t", j=TOPK))

            dve.wait_ge(lg_ready, 1)
            for t in range(T):
                mark(nc.vector.max(top[:, t, :], lg[:, t, :]))
            settle()
            for t in range(T):
                mark(nc.vector.max_index(topi[:, t, :], top[:, t, :], lg[:, t, :]))
            nc.vector.tensor_tensor(dlt[:, :], top[:, :, 1], top[:, :, 0], ALU.subtract).then_inc(dlt_ready, 1)
            settle()
            mark(nc.vector.tensor_copy(idxf[:, :, :], topi[:, :, 0:TOPK]))
            settle()
            mark(nc.vector.tensor_tensor(
                oh[:, :, :, :].rearrange("p t j e -> p (t j) e"),
                cst[:, C_IOTA:C_IOTA + E].unsqueeze(1).broadcast_to([P, T * TOPK, E]),
                idxf[:, :, :].rearrange("p t j -> p (t j)").unsqueeze(2).broadcast_to([P, T * TOPK, E]),
                ALU.is_equal))
            settle()
            nc.vector.tensor_tensor(mask[:, :, :], oh[:, :, 0, :], oh[:, :, 1, :], ALU.add).then_inc(mask_ready, 1)
            dve.wait_ge(ed_ready, 1)
            mark(nc.vector.tensor_scalar(ed1[:, :], ed[:, :], 1.0, None, ALU.add))
            settle()
            mark(nc.vector.reciprocal(pay[:, 0, :, D + 1], ed1[:, :]))
            settle()
            mark(nc.vector.tensor_tensor(pay[:, 1, :, D + 1], ed[:, :], pay[:, 0, :, D + 1], ALU.mult))

            dve.wait_ge(rank_ps, 1)
            rank = ps[:, 3, 3 * P:3 * P + T * E].rearrange("p (t e) -> p t e", t=T)
            cnt = ps[:, 2, 3 * P:3 * P + E]
            mark(nc.vector.tensor_tensor(ovm[:, :, :], cnt.unsqueeze(2).broadcast_to([P, E, MAXB - 1]),
                                         cst[:, C_THR:C_BLK].unsqueeze(1).broadcast_to([P, E, MAXB - 1]),
                                         ALU.is_gt))
            settle()
            mark(nc.vector.tensor_reduce(nov[:, :], ovm[:, :, :], AX_X, ALU.add))
            settle()
            mark(nc.vector.tensor_tensor_scan(novi[:, :], cst[:, C_ONE:C_ONE + E], nov[:, :], 0.0,
                                              ALU.mult, ALU.add))
            settle()
            mark(nc.vector.tensor_tensor(dif[:, :], novi[:, :], nov[:, :], ALU.subtract))
            settle()
            mark(nc.vector.tensor_scalar(dif2[:, :], dif[:, :], float(P), float((E - 1) * P), ALU.mult, ALU.add))
            settle()
            mark(nc.vector.tensor_tensor(dif[:, :], dif2[:, :], cst[:, C_EBASE:C_EBASE + E], ALU.subtract))
            mark(nc.vector.tensor_tensor(s2[:, :, :], rank,
                                         cst[:, C_EBASE:C_EBASE + E].unsqueeze(1).broadcast_to([P, T, E]), ALU.add))
            settle()
            mark(nc.vector.scalar_tensor_tensor(s1[:, :, :], rank, float(P),
                                                dif[:, :].unsqueeze(1).broadcast_to([P, T, E]),
                                                ALU.is_ge, ALU.mult))
            settle()
            mark(nc.vector.tensor_tensor(s3[:, :, :], s1[:, :, :], s2[:, :, :], ALU.add))
            settle()
            mark(nc.vector.tensor_tensor(s4[:, :, :, :], oh[:, :, :, :],
                                         s3[:, :, :].unsqueeze(2).broadcast_to([P, T, TOPK, E]), ALU.mult))
            settle()
            mark(nc.vector.tensor_reduce(slotf[:, :], s4[:, :, :, :].rearrange("p t j e -> p (t j) e"),
                                         AX_X, ALU.add))
            settle()
            nc.vector.tensor_copy(slot[:, :], slotf[:, :]).then_inc(slot_ready, 1)
            mark(nc.vector.tensor_copy(ctl[0:1, 0:1], novi[0:1, E - 1:E]))
            mark(nc.vector.tensor_tensor(
                eom[:, :, :], novi[0:1, :].unsqueeze(1).broadcast_to([1, NOV, E]),
                cst[0:1, C_BLK:C_BLK + NOV].unsqueeze(2).broadcast_to([1, NOV, E]), ALU.is_le))
            settle()
            mark(nc.vector.tensor_reduce(eof[:, :], eom[:, :, :], AX_X, ALU.add))
            settle()
            nc.vector.tensor_scalar(ctl[0:1, 1:1 + NOV], eof[:, :], float(E - 1), None,
                                    ALU.min).then_inc(ctl_ready, 1)

            def gated(u, e):
                b = u % 2
                dve.wait_ge(sg_ready, e + 1)
                nc.vector.tensor_tensor(hid[:, b, :], sg[:, b, :], ps[:, b, F:2 * F], ALU.mult).then_inc(hid_ready, 1)

            def evac_hidT(u, e):
                b = u % 2
                dve.wait_ge(hidT_ps, e + 1)
                nc.vector.tensor_copy(hidT[:, b, :, :].rearrange("p c s -> p (c s)"),
                                      ps[:, 3, 0:F]).then_inc(hidT_ready, 1)

            def result(u, e):
                dve.wait_ge(y_ps, e + 1)
                nc.vector.tensor_copy(yi[:, u:u + 1], xs[:, u, D:D + 1])
                nc.vector.tensor_scalar(ys[:, u, :], ps[:, 4, 0:D],
                                        xs[:, u, D + 1:D + 2], None, ALU.mult).then_inc(y_ready, 1)

            for u in range(NBUF):
                gated(u, u)
                evac_hidT(u, u)
                result(u, u)
            with dve.Fori(NBUF, E, NBUF) as e0:
                for u in range(NBUF):
                    gated(u, e0 + u)
                    evac_hidT(u, e0 + u)
                    dve.wait_ge(y_out[u], e0 * (16 // NBUF))
                    result(u, e0 + u)
            dve.wait_ge(ctl_ready, 1)
            n_over = dve.value_load(ctl[0:1, 0:1], min_val=0, max_val=NOV)
            dve.wait_ge(y_out[0], 16 * (E // NBUF))
            with dve.Fori(0, NOV) as i:
                with dve.If(i < n_over):
                    gated(0, i + E)
                    evac_hidT(0, i + E)
                    result(0, i + E)

            dve.wait_ge(yb_in, 16)
            mark(nc.vector.tensor_tensor(acc[:, :, :], h2[:, :, :], yb[:, 0, :, :], ALU.add))
            settle()
            nc.vector.tensor_tensor(fin[:, :, :], acc[:, :, :], yb[:, 1, :, :], ALU.add).then_inc(fin_ready, 1)

        @block.tensor
        def _(pe):
            mm = nc.tensor.matmul
            pe.wait_ge(in_first, 32)
            pe.wait_ge(in_small, 16 * N_SMALL)
            for t in range(T):
                o = ps[:, t, 0:D]
                for c in range(2):
                    a = (2 * t + c) * B
                    mm(o, xT[:, a:a + P], tokW[:, c, :], start=(c == 0), stop=False)
                mm(o, ones_row, rows[:, 0, :], start=False, stop=True).then_inc(proj_ready, 1)
            for t in range(T):
                pe.wait_ge(xn_ready, t + 1)
                nc.tensor.transpose(ps[:, t, P:2 * P], xn[:, t, :], ident).then_inc(xnT_ps, 1)
            pe.wait_ge(xnT_ready, T)
            for n in range(2):
                w = qkvW[:, n * D:(n + 1) * D]
                mm(ps[:, 2 * n, :], w, xnT[:, 0:8, 0, :], start=True, stop=True)
                mm(ps[:, 2 * n + 1, 0:TOK - 512], w, xnT[:, 8:S, 0, :], start=True, stop=True).then_inc(qk_ps, 1)
            for k in range(S):
                o = ps[:, 5 + k // 4, (k % 4) * D:(k % 4 + 1) * D]
                twice = xnT[:, k, :, :].rearrange("p r b -> p (r b)")
                mm(o, twice, qkvW[:, 2 * D:3 * D], start=True, stop=False)
                last = mm(o, ones_row, rows[:, 1, :], start=False, stop=True)
            last.then_inc(v_ps, 1)

            def scores(i):
                if i == 0:
                    pe.wait_ge(bias_ready, 1)
                o = ps[:, 4 * (1 - i % 2), 0:S * H]
                pe.wait_ge(prod_ready, i + 1)
                mm(o, cst[0:2, C_PAR:C_PAR + P], bias[:, i, :], start=True, stop=False, skip_group_check=True)
                for k in range(S):
                    last = mm(o[:, k * H:(k + 1) * H], prod[:, i % 2, k * P:(k + 1) * P],
                              cst[:, C_HEAD:C_HEAD + H], start=False, stop=(k == S - 1), skip_group_check=True)
                last.then_inc(scores_ps, 1)

            def heads_out(i):
                pe.wait_ge(pv_ready, i + 1)
                o = ps[:, 1 + i % 2, 0:P]
                for k in range(S):
                    last = mm(o, prodv[:, i % 2, k * D:(k + 1) * D], ident, start=(k == 0), stop=(k == S - 1))
                last.then_inc(o_ps, 1)

            def project(i):
                pe.wait_ge(oT_ready, i + 1)
                o = attn_out(i)
                mm(o, oT[:, i, :], outW[:, :], start=True, stop=False)
                mm(o, ones_row, rows[:, 2, :], start=False, stop=True).then_inc(a_ps, 1)

            for i in range(T + 3):
                if i < T:
                    scores(i)
                if 0 <= i - 2 < T:
                    heads_out(i - 2)
                if i >= 3:
                    project(i - 3)
            for t in range(T):
                pe.wait_ge(x2_ready, t + 1)
                nc.tensor.transpose(ps[:, X2_BANK[t], 0:P], pay[:, 0, t, 0:D],
                                    ident).then_inc(x2T_ps, 1)
            for t in range(T):
                pe.wait_ge(x2T_ready, t + 1)
                last = mm(ps[:, 4, t * E:(t + 1) * E], x2T[:, t, :], routeW[:, :], start=True, stop=True)
            last.then_inc(lg_ps, 1)
            pe.wait_ge(mask_ready, 1)
            m2 = mask[:, :, :].rearrange("p t e -> p (t e)")
            o = ps[:, 3, 3 * P:3 * P + T * E]
            mm(o, cst[:, C_TRI:C_TRI + P], m2, start=True, stop=False, skip_group_check=True)
            for n in range(1, T):
                mm(o[:, n * E:], cst[:, C_ONE:C_ONE + P], m2[:, 0:(T - n) * E], start=False, stop=(n == T - 1),
                   skip_group_check=True)
            for t in range(T):
                last = mm(ps[:, 2, 3 * P:3 * P + E], cst[:, C_ONE:C_ONE + P], mask[:, t, :],
                          start=(t == 0), stop=(t == T - 1))
            last.then_inc(rank_ps, 1)

            pe.wait_ge(in_expert, 16 * (E // NBUF))

            def rows_T(u, g):
                pe.wait_ge(xs_in[u], g)
                nc.tensor.transpose(ps[:, 2, 0:P], xs[:, u, 0:D], ident).then_inc(xsT_ps, 1)

            def gate_up(u, e, w):
                pe.wait_ge(xsT_ready, e + 1)
                mm(ps[:, u % 2, :], xsT[:, u % 2, :], w, start=True, stop=True).then_inc(g_ps, 1)

            def hidden_T(u, e):
                b = u % 2
                pe.wait_ge(hid_ready, e + 2)
                for c in range(2):
                    last = nc.tensor.transpose(ps[:, 3, c * P:(c + 1) * P],
                                               hid[:, b, c * P:(c + 1) * P], ident)
                last.then_inc(hidT_ps, 1)

            def down(u, e, w):
                b = u % 2
                pe.wait_ge(hidT_ready, e + 1)
                for c in range(2):
                    last = mm(ps[:, 4, 0:D], hidT[:, b, c, :], w(c), start=(c == 0), stop=(c == 1))
                last.then_inc(y_ps, 1)

            def up_w(e):
                return expW[:, bass.ds(e * WROW, 2 * F)]

            def down_w(e):
                return lambda c: expW[:, bass.ds(e * WROW + (2 * F + c * D), D)]

            rows_T(0, 16)
            gate_up(0, 0, up_w(0))

            def group(e0, last_group):
                for u in range(NBUF):
                    e = e0 + u
                    v = (u + 1) % NBUF
                    if not (last_group and u == NBUF - 1):
                        rows_T(v, e0 * (16 // NBUF) + (16 if v else 32))
                        pe.wait_ge(hid_ready, e + 1)
                        gate_up(v, e + 1, up_w(e + 1))
                    hidden_T(u, e)
                    down(u, e, down_w(e))

            with pe.Fori(0, E - NBUF, NBUF) as e0:
                group(e0, False)
            group(E - NBUF, True)
            pe.wait_ge(ctl_ready, 1)
            n_over = pe.value_load(ctl[0:1, 0:1], min_val=0, max_val=NOV)
            with pe.Fori(0, NOV) as i:
                with pe.If(i < n_over):
                    owner = pe.value_load(ctl[0:1, bass.ds(i + 1, 1)], min_val=0, max_val=E - 1)
                    rows_T(0, i * 16 + 16 * (E // NBUF + 1))
                    gate_up(0, i + E, up_w(owner))
                    hidden_T(0, i + E)
                    down(0, i + E, down_w(owner))


_ARGS = ["x_t", "tok_w", "tok_b", "gamma", "beta", "qkv_wt", "qk_b", "v_b", "out_wt", "out_b", "t_head",
         "router_wt", "expert_w", "table"]


def kernel(x, L0_tok_W, L0_tok_b, L0_tok_gamma, L0_tok_beta, L0_attn_in_proj_w, L0_attn_in_proj_b,
           L0_attn_out_proj_w, L0_attn_out_proj_b, L0_attn_t, L0_ffn_router_w, L0_ffn_gate_w,
           L0_ffn_up_w, L0_ffn_down_w):
    import numpy as _np
    import concourse.bacc as _bacc
    from concourse import mybir as _mybir
    from concourse.bass_utils import run_bass_kernel_spmd as _run

    a = _np.ascontiguousarray
    xf = _np.asarray(x).reshape(B, -1)[:, :CHUNKS * P]
    ex = [a(_np.asarray(L0_ffn_gate_w).transpose(1, 0, 2)),
          a(_np.asarray(L0_ffn_up_w).transpose(1, 0, 2)),
          a(_np.asarray(L0_ffn_down_w).reshape(E, 2, P, D).transpose(2, 0, 1, 3).reshape(P, E, 2 * D))]
    inb = _np.asarray(L0_attn_in_proj_b)
    data = {
        "x_t": a(xf.reshape(B, CHUNKS, P).transpose(2, 1, 0).reshape(P, CHUNKS * B)),
        "tok_w": a(_np.asarray(L0_tok_W).reshape(2, P, D).transpose(1, 0, 2)),
        "tok_b": _np.asarray(L0_tok_b).reshape(1, D),
        "gamma": _np.asarray(L0_tok_gamma),
        "beta": _np.asarray(L0_tok_beta),
        "qkv_wt": a(_np.asarray(L0_attn_in_proj_w).T),
        "qk_b": a(inb[:2 * D].reshape(2, D).T),
        "v_b": a(inb[2 * D:]).reshape(1, D),
        "out_wt": a(_np.asarray(L0_attn_out_proj_w).T),
        "out_b": _np.asarray(L0_attn_out_proj_b).reshape(1, D),
        "t_head": _np.asarray(L0_attn_t),
        "router_wt": a(_np.asarray(L0_ffn_router_w).T),
        "expert_w": a(_np.concatenate(ex, axis=2).reshape(P, E * WROW)),
        "table": constants(),
    }
    nc = _bacc.Bacc("TRN2", target_bir_lowering=False, num_devices=1)
    arrays, args = {}, []
    for name in _ARGS:
        v = a(data[name])
        arrays[name + "_dram"] = v
        args.append(nc.dram_tensor(name + "_dram", v.shape, _mybir.dt.from_np(v.dtype), kind="ExternalInput").ap())
    out = nc.dram_tensor("out_dram", (B, S, D), _mybir.dt.float32, kind="ExternalOutput").ap()
    audio_tower(nc, *args, out)
    r = _run(nc, [arrays], core_ids=[0])
    return r.results[0]["out_dram"]
```

```python
from contextlib import ExitStack

import numpy as np

import concourse.bass as bass
from concourse import mybir

F32 = mybir.dt.float32
U32 = mybir.dt.uint32
I32 = mybir.dt.int32
ALU = mybir.AluOpType
ACT = mybir.ActivationFunctionType
AX_X = mybir.AxisListType.X

P = 128
B = 64
S = 10
T = S // 2
D = 128
H = 8
DH = D // H
E = 16
F = 256
TOPK = 2
TOK = B * S
CHUNKS = S + 1
WROW = 2 * F + F
MAXB = TOK // P
NOV = (TOK * TOPK - E) // P
BLK = E + 1
ROWS = E * TOK
ROW = D + 2
NBUF = 4
FILL = 10
EPS_TOK = 1e-3
EPS_LN = 1e-5
FAR = -1e30

C_ID = 0
C_TRI = C_ID + P
C_ONE = C_TRI + P
C_HEAD = C_ONE + P
C_IOTA = C_HEAD + H
C_EBASE = C_IOTA + E
C_PAR = C_EBASE + E
C_DIST = C_PAR + P
C_HALF = C_DIST + T * S
C_THR = C_HALF + T
C_BLK = C_THR + MAXB - 1
C_DST = C_BLK + NOV
C_WQKV = C_DST + TOPK * T
C_WOUT = C_WQKV + 3 * D
C_WROUTE = C_WOUT + D
C_BQKV = C_WROUTE + E
C_END = C_BQKV + 3


def constants():
    p = np.arange(P)
    c = np.zeros((P, C_WQKV), np.float32)
    c[:, C_ID:C_ID + P] = np.eye(P)
    c[:, C_TRI:C_TRI + P] = p[:, None] < p[None, :]
    c[:, C_ONE:C_ONE + P] = 1.0
    c[:, C_HEAD:C_HEAD + H] = (p[:, None] // DH == np.arange(H)[None, :]) * DH ** -0.5
    c[:, C_IOTA:C_IOTA + E] = np.arange(E)
    c[:, C_EBASE:C_EBASE + E] = np.arange(E) * TOK
    c[0:2, C_PAR:C_PAR + P] = np.arange(2)[:, None] == p[None, :] // B
    q = 2 * np.arange(T)[None, :, None] + np.arange(2)[:, None, None]
    c[0:2, C_DIST:C_DIST + T * S] = (-(q - np.arange(S)[None, None, :]) ** 2.0).reshape(2, T * S)
    c[:, C_HALF:C_HALF + T] = -0.5
    c[:, C_THR:C_THR + MAXB - 1] = P * np.arange(1, MAXB)
    c[:, C_BLK:C_BLK + NOV] = np.arange(NOV)
    dst = P * (TOPK * np.arange(T)[None, :] + np.arange(TOPK)[:, None])
    c[:, C_DST:C_WQKV] = dst.reshape(1, -1) + p[:, None]
    return c


def audio_tower(nc, first, rows_d, gb, t_head, table, expert_w, out):
    with ExitStack() as ctx:
        def sb(name, shape, dt=F32):
            return ctx.enter_context(nc.sbuf_tensor(name, shape, dt))

        def sem(name):
            return ctx.enter_context(nc.semaphore(name))

        ps = ctx.enter_context(nc.psum_tensor("ps", [P, 8, 512], F32))

        xw = sb("xw", [P, CHUNKS * B + 2 * D])
        xT = xw[:, 0:CHUNKS * B]
        tokW = xw[:, CHUNKS * B:].rearrange("p (c d) -> p c d", c=2)
        tokB = sb("tokB", [1, D])
        ones1 = sb("ones1", [1, P])
        gbo = sb("gbo", [P, 3, D])
        headT = sb("headT", [2, H])
        cst = sb("cst", [P, C_END])
        expW = sb("expW", [P, E * WROW])

        stats = sb("stats", [P, T, 6])
        mv = sb("mv", [P, T, 2])
        mve = sb("mve", [P, T])
        rstd = sb("rstd", [P, T])
        pg = sb("pg", [P, T, D])
        h = sb("h", [P, T, D])
        hb = sb("hb", [P, T, D])
        xn = sb("xn", [P, T, D])
        xnT = sb("xnT", [P, S, 2, B])
        qT = sb("qT", [P, TOK])
        kT = sb("kT", [P, TOK])
        sig = sb("sig", [2, 4, H])
        bias = sb("bias", [2, T, S * H])
        prod = sb("prod", [P, T, S * P])
        mx = sb("mx", [P, 2, H])
        sc = sb("sc", [P, 2, S * H])
        ex = sb("ex", [P, 2, S * H])
        den = sb("den", [P, 2, H])
        rden = sb("rden", [P, 2, H])
        pn = sb("pn", [P, 2, S * H])
        prodv = sb("prodv", [P, 2, S * D])
        oT = sb("oT", [P, T, P])
        h2 = sb("h2", [P, T, D])
        pay = sb("pay", [P, TOPK, T, ROW])
        x2T = sb("x2T", [P, T, P])
        top = sb("top", [P, T, 8])
        topi = sb("topi", [P, T, 8], U32)
        idxf = sb("idxf", [P, T, TOPK])
        oh = sb("oh", [P, T, TOPK, E])
        mask = sb("mask", [P, T, E])
        cum = sb("cum", [P, T + 1, E])
        dlt = sb("dlt", [P, T])
        ed = sb("ed", [P, T])
        ed1 = sb("ed1", [P, T])
        srow = sb("srow", [P, T, E])
        spick = sb("spick", [P, T, TOPK, E])
        slotf = sb("slotf", [P, T, TOPK])
        slot = sb("slot", [P, T, TOPK], U32)
        ovm = sb("ovm", [1, E, MAXB - 1])
        nov = sb("nov", [1, E])
        novi = sb("novi", [1, E])
        eom = sb("eom", [1, NOV, E])
        eov = sb("eov", [1, NOV, E])
        eof = sb("eof", [1, NOV])
        eof2 = sb("eof2", [1, NOV])
        eob = sb("eob", [1, NOV])
        eor = sb("eor", [1, NOV])
        eor2 = sb("eor2", [1, NOV])
        ctl = sb("ctl", [1, 1 + 2 * NOV], I32)
        blank = sb("blank", [P, FILL, ROW])
        xs = sb("xs", [P, NBUF, ROW])
        meta = sb("meta", [P, BLK + NOV, 2])
        xsT = sb("xsT", [P, 2, P])
        sg = sb("sg", [P, 2, F])
        hid = sb("hid", [P, 2, F])
        hidT = sb("hidT", [P, 2, 2, P])
        ys = sb("ys", [P, NBUF, D])
        yi = sb("yi", [P, NBUF], U32)
        yb = sb("yb", [P, T, TOPK, D])
        acc = sb("acc", [P, T, D])
        fin = sb("fin", [P, T, D])

        disp = nc.dram_tensor("disp", [ROWS, ROW], F32).ap()
        ybuf = nc.dram_tensor("ybuf", [TOPK * TOK, D], F32).ap()

        in_first = sem("in_first")
        in_rows = sem("in_rows")
        in_ln = sem("in_ln")
        in_head = sem("in_head")
        in_table = sem("in_table")
        in_expert = sem("in_expert")
        ones_set = sem("ones_set")
        s_blank = sem("s_blank")
        s_filled = sem("s_filled")
        dv = sem("dv")
        var_ready = sem("var_ready")
        rstd_ready = sem("rstd_ready")
        proj_ps = sem("proj_ps")
        h_ready = sem("h_ready")
        hb_ready = sem("hb_ready")
        xn_ready = sem("xn_ready")
        xnT_ps = sem("xnT_ps")
        xnT_ready = sem("xnT_ready")
        qk_ps = sem("qk_ps")
        qk_ready = sem("qk_ready")
        v_ps = sem("v_ps")
        bias_ready = sem("bias_ready")
        prod_ready = sem("prod_ready")
        scores_ps = sem("scores_ps")
        sub_ready = sem("sub_ready")
        exp_ready = sem("exp_ready")
        pv_ready = sem("pv_ready")
        o_ps = sem("o_ps")
        oT_ready = sem("oT_ready")
        a_ps = sem("a_ps")
        x2_ready = sem("x2_ready")
        pay_ready = sem("pay_ready")
        x2T_ps = sem("x2T_ps")
        x2T_ready = sem("x2T_ready")
        lg_ps = sem("lg_ps")
        dlt_ready = sem("dlt_ready")
        ed_ready = sem("ed_ready")
        mask_ready = sem("mask_ready")
        rank_ps = sem("rank_ps")
        cnt_ps = sem("cnt_ps")
        slot_ready = sem("slot_ready")
        ctl_ready = sem("ctl_ready")
        s_disp = sem("s_disp")
        xs_in = [sem(f"xs_in{u}") for u in range(NBUF)]
        xs_over = sem("xs_over")
        xs_used = sem("xs_used")
        xsT_ps = sem("xsT_ps")
        xsT_ready = sem("xsT_ready")
        g_ps = sem("g_ps")
        sg_ready = sem("sg_ready")
        hid_ready = sem("hid_ready")
        hidT_ps = sem("hidT_ps")
        hidT_ready = sem("hidT_ready")
        y_ps = sem("y_ps")
        y_ready = sem("y_ready")
        y_taken = sem("y_taken")
        y_out = [sem(f"y_out{u}") for u in range(NBUF)]
        y_over = sem("y_over")
        over_done = sem("over_done")
        yb_in = [sem(f"yb_in{n}") for n in range(2)]
        fin_ready = sem("fin_ready")
        s_out = sem("s_out")

        ident = cst[:, C_ID:C_ID + P]
        outW = cst[:, C_WOUT:C_WOUT + D]
        routeW = cst[:, C_WROUTE:C_WROUTE + E]

        SCORES = (0, 4)
        HEADS, ROUTE, ATTN = 1, 2, 3
        VALUES = 5
        GATE, ROWS_T, HID_T, RESULT = (0, 1), 2, (3, 5), (4, 6)
        HALVES = ((0, 3), (3, T))

        block = ctx.enter_context(nc.Block())

        @block.sync
        def _(sp):
            sp.dma_start(xw[:, :], first).then_inc(in_first, 16)
            sp.dma_start(tokB[:, :], rows_d).then_inc(in_rows, 16)
            sp.dma_start(headT[:, :], t_head.partition_broadcast(2)).then_inc(in_head, 16)
            sp.wait_ge(s_blank, 2)
            sp.dma_start(disp.rearrange("(p n r) c -> p n (r c)", p=P, r=FILL),
                         blank[:, :, :].rearrange("p r c -> p (r c)").unsqueeze(1)
                         .broadcast_to([P, ROWS // P // FILL, FILL * ROW])).then_inc(s_filled, 16)
            for g in range(0, E, NBUF):
                sp.dma_start(expW[:, g * WROW:(g + NBUF) * WROW],
                             expert_w[:, g * WROW:(g + NBUF) * WROW]).then_inc(in_expert, 16)

            sp.wait_ge(s_disp, 16 * T * TOPK)
            for u in range(NBUF):
                sp.dma_start(xs[:, u, :], disp[u * TOK:u * TOK + P, :]).then_inc(xs_in[u], 16)
            with sp.Fori(1, E // NBUF) as g:
                for u in range(NBUF):
                    row = sp.snap((g * NBUF + u) * TOK)
                    sp.wait_ge(xs_used, g * NBUF + (u - NBUF + 1))
                    sp.dma_start(xs[:, u, :], disp[bass.ds(row, P), :]).then_inc(xs_in[u], 16)
            sp.wait_ge(ctl_ready, 1)
            n_over = sp.value_load(ctl[0:1, 0:1], min_val=0, max_val=NOV)
            row = sp.value_load(ctl[0:1, 1 + NOV:2 + NOV], min_val=0, max_val=ROWS // P - 1) * P
            sp.wait_ge(xs_used, E - NBUF + 1)
            sp.dma_start(xs[:, 0, :], disp[bass.ds(row, P), :]).then_inc(xs_in[0], 16)
            with sp.If(n_over > 1):
                with sp.Fori(1, NOV) as i:
                    with sp.If(i < n_over):
                        row = sp.snap(sp.value_load(ctl[0:1, bass.ds(i + (1 + NOV), 1)],
                                                    min_val=0, max_val=ROWS // P - 1) * P)
                        sp.wait_ge(y_ready, i + E)
                        sp.dma_start(xs[:, 0, :], disp[bass.ds(row, P), :]).then_inc(xs_over, 16)
                        sp.wait_ge(y_over, i * 16)
                        sp.sem_inc(over_done, 1)

            for u in range(NBUF):
                sp.wait_ge(y_out[u], 16 * (E // NBUF + (u == 0)))
            yv = ybuf.rearrange("(t j p) c -> p t j c", j=TOPK, p=P)
            for n, (a, b) in enumerate(HALVES):
                sp.dma_start(yb[:, a:b, :, :], yv[:, a:b, :, :]).then_inc(yb_in[n], 16)
            ov = out.rearrange("b (t r) d -> r b t d", r=2)
            for n, (a, b) in enumerate(HALVES):
                sp.wait_ge(fin_ready, n + 1)
                sp.dma_start(ov[0][:, a:b, :], fin[0:B, a:b, :]).then_inc(s_out, 16)
            sp.wait_ge(s_out, 16 * 4)

        @block.gpsimd
        def _(pool):
            nc.gpsimd.memset(blank[:, :, :], 0.0).then_inc(s_blank, 1)
            pool.wait_ge(s_blank, 1)
            nc.gpsimd.memset(blank[:, :, D:D + 1], float(4 * TOPK * TOK)).then_inc(s_blank, 1)
            pool.wait_ge(in_table, 16)

            def power(n, a, b):
                pool.wait_ge(var_ready, n)
                nc.gpsimd.tensor_tensor(rstd[:, a:b], mve[:, a:b], cst[:, C_HALF + a:C_HALF + b],
                                        ALU.pow).then_inc(rstd_ready, 1)

            power(1, 0, T)
            power(2, 0, T)
            pool.wait_ge(in_ln, 16)
            pool.wait_ge(h_ready, 1)
            nc.gpsimd.tensor_tensor(hb[:, :, :], h[:, :, :], gbo[:, 2, :].unsqueeze(1).broadcast_to([P, T, D]),
                                    ALU.add).then_inc(hb_ready, 1)

            def products(i):
                nc.gpsimd.tensor_tensor(
                    prod[:, i, :].rearrange("p (k r b) -> p k r b", k=S, r=2),
                    qT[:, i * P:(i + 1) * P].rearrange("p (r b) -> p r b", r=2).unsqueeze(1)
                    .broadcast_to([P, S, 2, B]),
                    kT[:, :].rearrange("p (k b) -> p k b", k=S).unsqueeze(2).broadcast_to([P, S, 2, B]),
                    ALU.mult).then_inc(prod_ready, 1)

            pool.wait_ge(qk_ready, 2)
            for i in range(T):
                products(i)
            pool.wait_ge(s_filled, 16)
            for i in range(T + 1):
                if i < T:
                    power(3 + i, i, i + 1)
                if i >= 1:
                    t = i - 1
                    pool.wait_ge(slot_ready, t + 1)
                    pool.wait_ge(pay_ready, t + 1)
                    for j in range(TOPK):
                        nc.gpsimd.indirect_dma_start(
                            out=disp, out_offset=bass.IndirectOffsetOnAxis(ap=slot[:, t, j:j + 1], axis=0),
                            in_=pay[:, j, t, :], in_offset=None).then_inc(s_disp, 16)

            def scatter(u, done):
                nc.gpsimd.indirect_dma_start(
                    out=ybuf, out_offset=bass.IndirectOffsetOnAxis(ap=yi[:, u:u + 1], axis=0),
                    in_=ys[:, u, :], in_offset=None, bounds_check=TOPK * TOK - 1,
                    oob_is_err=False).then_inc(done, 16)

            with pool.Fori(0, E // NBUF) as g:
                for u in range(NBUF):
                    pool.wait_ge(y_ready, g * NBUF + (u + 1))
                    pool.sem_inc(y_taken, 1)
                    scatter(u, y_out[u])
            pool.wait_ge(y_ready, BLK)
            scatter(0, y_out[0])
            n_over = pool.value_load(ctl[0:1, 0:1], min_val=0, max_val=NOV)
            with pool.If(n_over > 1):
                with pool.Fori(1, NOV) as i:
                    with pool.If(i < n_over):
                        pool.wait_ge(y_ready, i + BLK)
                        pool.sem_inc(y_taken, 1)
                        scatter(1, y_over)

        @block.scalar
        def _(act):
            act.dma_start(cst[:, :], table).then_inc(in_table, 16)
            act.dma_start(gbo[:, :, :].rearrange("p a d -> p (a d)"), gb.partition_broadcast(P)).then_inc(in_ln, 16)
            act.wait_ge(in_table, 16)
            for t in range(T):
                act.wait_ge(xnT_ps, t + 1)
                nc.scalar.copy(xnT[:, 2 * t:2 * t + 2, :, :],
                               ps[:, t, P:2 * P].rearrange("p (r b) -> p r b", r=2).unsqueeze(2)
                               .broadcast_to([P, 2, 2, B])).then_inc(xnT_ready, 1)
            for n, dst in enumerate((kT, qT)):
                act.wait_ge(qk_ps, n + 1)
                nc.scalar.activation(dst[:, :], ps[:, 2 * n:2 * n + 2, :].rearrange("p a b -> p (a b)")[:, 0:TOK],
                                     ACT.Identity, bias=cst[:, C_BQKV + 1 - n:C_BQKV + 2 - n]).then_inc(qk_ready, 1)

            for j in range(T + 2):
                if j < T:
                    act.wait_ge(sub_ready, j + 1)
                    nc.scalar.activation(ex[:, j % 2, :], sc[:, j % 2, :], ACT.Exp).then_inc(exp_ready, 1)
                if j >= 2:
                    t = j - 2
                    act.wait_ge(x2T_ps, t + 1)
                    nc.scalar.copy(x2T[:, t, :], ps[:, ROUTE, 0:P]).then_inc(x2T_ready, 1)
                    act.wait_ge(x2_ready, t + 1)
                    nc.scalar.copy(pay[:, 1, t, 0:D], pay[:, 0, t, 0:D]).then_inc(pay_ready, 1)
                    act.wait_ge(dlt_ready, t + 1)
                    nc.scalar.activation(ed[:, t:t + 1], dlt[:, t:t + 1], ACT.Exp).then_inc(ed_ready, 1)
                if j < T:
                    act.wait_ge(o_ps, j + 1)
                    nc.scalar.activation(oT[:, j, :], ps[:, HEADS, 0:P], ACT.Identity,
                                         bias=cst[:, C_BQKV + 2:C_BQKV + 3]).then_inc(oT_ready, 1)

            def take_rows(b, src, e):
                act.wait_ge(xsT_ps, e + 1)
                nc.scalar.copy(xsT[:, b, :], ps[:, ROWS_T, 0:P]).then_inc(xsT_ready, 1)
                nc.scalar.copy(meta[:, bass.ds(e, 1), :].rearrange("p a c -> p (a c)"),
                               xs[:, src, D:ROW]).then_inc(xs_used, 1)

            def silu(b, e):
                act.wait_ge(g_ps, e + 1)
                nc.scalar.activation(sg[:, b, :], ps[:, GATE[b], 0:F], ACT.Silu).then_inc(sg_ready, 1)

            take_rows(0, 0, 0)
            with act.Fori(0, E // NBUF) as g:
                for u in range(NBUF):
                    take_rows((u + 1) % 2, (u + 1) % NBUF, g * NBUF + (u + 1))
                    silu(u % 2, g * NBUF + u)
            silu(0, E)
            n_over = act.value_load(ctl[0:1, 0:1], min_val=0, max_val=NOV)
            with act.If(n_over > 1):
                with act.Fori(1, NOV) as i:
                    with act.If(i < n_over):
                        take_rows(0, 0, i + E)
                        silu(0, i + E)
            ov = out.rearrange("b (t r) d -> r b t d", r=2)
            for n, (a, b) in enumerate(HALVES):
                act.wait_ge(fin_ready, n + 1)
                act.dma_start(ov[1][:, a:b, :], fin[B:P, a:b, :]).then_inc(s_out, 16)

        @block.vector
        def _(dve):
            count = [0]

            def mark(ins):
                count[0] += 1
                ins.then_inc(dv, 1)
                return count[0]

            def need(step):
                dve.wait_ge(dv, step)

            nc.vector.memset(ones1[:, :], 1.0).then_inc(ones_set, 1)
            nc.vector.memset(ctl[:, :], 0).then_inc(hid_ready, 1)
            nc.vector.memset(cum[:, 0, :], 0.0)
            dve.wait_ge(in_head, 16)
            need(mark(nc.vector.tensor_tensor(sig[:, 0, :], headT[:, :], headT[:, :], ALU.mult)))
            need(mark(nc.vector.scalar_tensor_tensor(sig[:, 1, :], sig[:, 0, :], 2.0, sig[:, 0, :],
                                                     ALU.mult, ALU.mult)))
            need(mark(nc.vector.tensor_scalar(sig[:, 2, :], sig[:, 1, :], 1e-37, None, ALU.max)))
            need(mark(nc.vector.reciprocal(sig[:, 3, :], sig[:, 2, :])))
            dve.wait_ge(in_table, 16)
            need(mark(nc.vector.tensor_tensor(
                bias[:, :, :].rearrange("r t (k h) -> r (t k) h", h=H),
                cst[0:2, C_DIST:C_DIST + T * S].unsqueeze(2).broadcast_to([2, T * S, H]),
                sig[:, 3, :].unsqueeze(1).broadcast_to([2, T * S, H]), ALU.mult)))
            nc.vector.tensor_scalar(bias[:, :, :], bias[:, :, :], FAR, None, ALU.max).then_inc(bias_ready, 1)
            nc.vector.tensor_copy(pay[:, :, :, D], cst[:, C_DST:C_WQKV].rearrange("p (j t) -> p j t", j=TOPK))

            dve.wait_ge(in_ln, 16)
            for t in range(T):
                dve.wait_ge(proj_ps, t + 1)
                need(mark(nc.vector.bn_stats(stats[:, t, :], ps[:, t, 0:D])))
                got = mark(nc.vector.bn_aggr(mv[:, t, :], stats[:, t, :]))
                need(got)
                if t < T - 1:
                    centred = mark(nc.vector.scalar_tensor_tensor(pg[:, t, :], ps[:, t, 0:D], mv[:, t, 0:1],
                                                                  gbo[:, 0, :], ALU.subtract, ALU.mult))
            nc.vector.tensor_scalar(mve[:, :], mv[:, :, 1], EPS_TOK, None, ALU.add).then_inc(var_ready, 1)
            centred = mark(nc.vector.scalar_tensor_tensor(pg[:, T - 1, :], ps[:, T - 1, 0:D], mv[:, T - 1, 0:1],
                                                          gbo[:, 0, :], ALU.subtract, ALU.mult))
            dve.wait_ge(rstd_ready, 1)
            need(centred)
            for t in range(T):
                scaled = mark(nc.vector.scalar_tensor_tensor(h[:, t, :], pg[:, t, :], rstd[:, t:t + 1],
                                                             gbo[:, 1, :], ALU.mult, ALU.add))
            need(scaled)
            nc.vector.sem_inc(h_ready, 1)
            for t in range(T):
                got = mark(nc.vector.bn_stats(stats[:, t, :], h[:, t, :]))
            need(got)
            for t in range(T):
                got = mark(nc.vector.bn_aggr(mv[:, t, :], stats[:, t, :]))
            need(got)
            nc.vector.tensor_scalar(mve[:, :], mv[:, :, 1], EPS_LN, None, ALU.add).then_inc(var_ready, 1)
            dve.wait_ge(rstd_ready, 2)
            for t in range(T):
                nc.vector.tensor_scalar(xn[:, t, :], h[:, t, :], mv[:, t, 0:1], rstd[:, t:t + 1],
                                        ALU.subtract, ALU.mult).then_inc(xn_ready, 1)

            v_all = ps[:, VALUES:VALUES + 3, :].rearrange("p a b -> p (a b)")[:, 0:S * D]

            def minus_max(i):
                b = i % 2
                dve.wait_ge(scores_ps, i + 1)
                s = ps[:, SCORES[b], 0:S * H]
                need(mark(nc.vector.tensor_reduce(mx[:, b, :], s.rearrange("p (k h) -> p h k", h=H), AX_X, ALU.max)))
                nc.vector.tensor_tensor(
                    sc[:, b, :].rearrange("p (k h) -> p k h", h=H), s.rearrange("p (k h) -> p k h", h=H),
                    mx[:, b, :].unsqueeze(1).broadcast_to([P, S, H]), ALU.subtract).then_inc(sub_ready, 1)

            def weighted_values(i):
                b = i % 2
                dve.wait_ge(exp_ready, i + 1)
                need(mark(nc.vector.tensor_reduce(den[:, b, :], ex[:, b, :].rearrange("p (k h) -> p h k", h=H),
                                                  AX_X, ALU.add)))
                need(mark(nc.vector.reciprocal(rden[:, b, :], den[:, b, :])))
                need(mark(nc.vector.tensor_tensor(
                    pn[:, b, :].rearrange("p (k h) -> p k h", h=H),
                    ex[:, b, :].rearrange("p (k h) -> p k h", h=H),
                    rden[:, b, :].unsqueeze(1).broadcast_to([P, S, H]), ALU.mult)))
                if i == 0:
                    dve.wait_ge(v_ps, 1)
                if i >= 2:
                    dve.wait_ge(o_ps, i - 1)
                nc.vector.tensor_tensor(
                    prodv[:, b, :].rearrange("p (n d) -> p n d", d=DH),
                    v_all.rearrange("p (n d) -> p n d", d=DH),
                    pn[:, b, :].unsqueeze(2).broadcast_to([P, S * H, DH]), ALU.mult).then_inc(pv_ready, 1)

            def residual(i):
                dve.wait_ge(a_ps, i + 1)
                if i == 0:
                    dve.wait_ge(hb_ready, 1)
                need(mark(nc.vector.tensor_tensor(h2[:, i, :], ps[:, ATTN, 0:D], hb[:, i, :], ALU.add)))
                need(mark(nc.vector.bn_stats(stats[:, i, :], h2[:, i, :])))
                need(mark(nc.vector.bn_aggr(mv[:, i, :], stats[:, i, :])))
                nc.vector.tensor_scalar(mve[:, i:i + 1], mv[:, i, 1:2], EPS_LN, None, ALU.add).then_inc(var_ready, 1)

            def normalise(i):
                dve.wait_ge(rstd_ready, 3 + i)
                nc.vector.tensor_scalar(pay[:, 0, i, 0:D], h2[:, i, :], mv[:, i, 0:1], rstd[:, i:i + 1],
                                        ALU.subtract, ALU.mult).then_inc(x2_ready, 1)

            def route(i):
                dve.wait_ge(lg_ps, i + 1)
                lg = ps[:, ROUTE, P:P + E]
                need(mark(nc.vector.max(top[:, i, :], lg)))
                found = mark(nc.vector.max_index(topi[:, i, :], top[:, i, :], lg))
                nc.vector.tensor_tensor(dlt[:, i:i + 1], top[:, i, 1:2], top[:, i, 0:1],
                                        ALU.subtract).then_inc(dlt_ready, 1)
                need(found)
                need(mark(nc.vector.tensor_copy(idxf[:, i, :], topi[:, i, 0:TOPK])))
                need(mark(nc.vector.tensor_tensor(
                    oh[:, i, :, :], cst[:, C_IOTA:C_IOTA + E].unsqueeze(1).broadcast_to([P, TOPK, E]),
                    idxf[:, i, :].unsqueeze(2).broadcast_to([P, TOPK, E]), ALU.is_equal)))
                nc.vector.tensor_tensor(mask[:, i, :], oh[:, i, 0, :], oh[:, i, 1, :], ALU.add).then_inc(mask_ready, 1)

            def slots(i):
                dve.wait_ge(ed_ready, i + 1)
                one = mark(nc.vector.tensor_scalar(ed1[:, i:i + 1], ed[:, i:i + 1], 1.0, None, ALU.add))
                dve.wait_ge(rank_ps, i + 1)
                at = mark(nc.vector.tensor_tensor(srow[:, i, :], ps[:, ROUTE, P + E:P + 2 * E],
                                                  cst[:, C_EBASE:C_EBASE + E], ALU.add))
                need(one)
                best = mark(nc.vector.reciprocal(pay[:, 0, i, D + 1:ROW], ed1[:, i:i + 1]))
                need(at)
                picked = mark(nc.vector.tensor_tensor(spick[:, i, :, :], oh[:, i, :, :],
                                                      srow[:, i, :].unsqueeze(1).broadcast_to([P, TOPK, E]),
                                                      ALU.mult))
                need(best)
                mark(nc.vector.tensor_tensor(pay[:, 1, i, D + 1:ROW], ed[:, i:i + 1], pay[:, 0, i, D + 1:ROW],
                                             ALU.mult))
                need(picked)
                need(mark(nc.vector.tensor_reduce(slotf[:, i, :], spick[:, i, :, :], AX_X, ALU.add)))
                mark(nc.vector.tensor_tensor(cum[:, i + 1, :], cum[:, i, :], mask[:, i, :], ALU.add))
                nc.vector.tensor_copy(slot[:, i, :], slotf[:, i, :]).then_inc(slot_ready, 1)

            for j in range(T + 2):
                if j < T:
                    minus_max(j)
                if j >= 2:
                    normalise(j - 2)
                if j < T:
                    weighted_values(j)
                if j >= 2:
                    route(j - 2)
                if 1 <= j <= T:
                    residual(j - 1)
                if j >= 2:
                    slots(j - 2)

            dve.wait_ge(cnt_ps, 1)
            cnt = ps[0:1, ROUTE, P + 2 * E:P + 3 * E]
            need(mark(nc.vector.tensor_tensor(ovm[:, :, :], cnt.unsqueeze(2).broadcast_to([1, E, MAXB - 1]),
                                              cst[0:1, C_THR:C_BLK].unsqueeze(1).broadcast_to([1, E, MAXB - 1]),
                                              ALU.is_gt)))
            need(mark(nc.vector.tensor_reduce(nov[:, :], ovm[:, :, :], AX_X, ALU.add)))
            need(mark(nc.vector.tensor_tensor_scan(novi[:, :], cst[0:1, C_ONE:C_ONE + E], nov[:, :], 0.0,
                                                   ALU.mult, ALU.add)))
            mark(nc.vector.tensor_copy(ctl[0:1, 0:1], novi[0:1, E - 1:E]))
            need(mark(nc.vector.tensor_tensor(
                eom[:, :, :], novi[0:1, :].unsqueeze(1).broadcast_to([1, NOV, E]),
                cst[0:1, C_BLK:C_BLK + NOV].unsqueeze(2).broadcast_to([1, NOV, E]), ALU.is_le)))
            mark(nc.vector.tensor_tensor(eov[:, :, :], eom[:, :, :], nov[0:1, :].unsqueeze(1)
                                         .broadcast_to([1, NOV, E]), ALU.mult))
            need(mark(nc.vector.tensor_reduce(eof[:, :], eom[:, :, :], AX_X, ALU.add)))
            mark(nc.vector.tensor_reduce(eob[:, :], eov[:, :, :], AX_X, ALU.add))
            need(mark(nc.vector.tensor_scalar(eof2[:, :], eof[:, :], float(E - 1), None, ALU.min)))
            mark(nc.vector.tensor_copy(ctl[0:1, 1:1 + NOV], eof2[:, :]))
            need(mark(nc.vector.scalar_tensor_tensor(eor[:, :], eof2[:, :], float(MAXB), cst[0:1, C_BLK:C_BLK + NOV],
                                                     ALU.mult, ALU.add)))
            need(mark(nc.vector.tensor_tensor(eor2[:, :], eor[:, :], eob[:, :], ALU.subtract)))
            need(mark(nc.vector.tensor_scalar(eor[:, :], eor2[:, :], 1.0, float(ROWS // P - 1), ALU.add, ALU.min)))
            need(mark(nc.vector.tensor_copy(ctl[0:1, 1 + NOV:], eor[:, :])))
            nc.vector.sem_inc(ctl_ready, 1)

            def gated(b, e):
                dve.wait_ge(sg_ready, e + 1)
                nc.vector.tensor_tensor(hid[:, b, :], sg[:, b, :], ps[:, GATE[b], F:2 * F],
                                        ALU.mult).then_inc(hid_ready, 1)

            def take_hidden(b, e):
                dve.wait_ge(hidT_ps, e + 1)
                nc.vector.tensor_copy(hidT[:, b, :, :].rearrange("p c s -> p (c s)"),
                                      ps[:, HID_T[b], 0:F]).then_inc(hidT_ready, 1)

            def result(b, u, e):
                dve.wait_ge(y_ps, e + 1)
                nc.vector.tensor_copy(yi[:, u:u + 1], meta[:, bass.ds(e, 1), 0:1].rearrange("p a c -> p (a c)"))
                nc.vector.tensor_scalar(ys[:, u, :], ps[:, RESULT[b], 0:D],
                                        meta[:, bass.ds(e, 1), 1:2].rearrange("p a c -> p (a c)"), None,
                                        ALU.mult).then_inc(y_ready, 1)

            for e in range(NBUF + 1):
                gated(e % 2, e)
                take_hidden(e % 2, e)
                if e >= 1:
                    result((e - 1) % 2, (e - 1) % NBUF, e - 1)

            def later(k, e):
                gated((k + 1) % 2, e)
                take_hidden((k + 1) % 2, e)
                dve.wait_ge(y_out[k], (e - (k + 1)) * (16 // NBUF))
                result(k % 2, k, e - 1)

            with dve.Fori(1, E // NBUF - 1) as g:
                for k in range(NBUF):
                    later(k, g * NBUF + (k + 1))
            for k in range(NBUF):
                later(k, E - NBUF + 1 + k)
            dve.wait_ge(y_out[0], 16 * (E // NBUF))
            result(0, 0, E)
            n_over = dve.value_load(ctl[0:1, 0:1], min_val=0, max_val=NOV)
            dve.wait_ge(y_out[1], 16 * (E // NBUF))
            with dve.If(n_over > 1):
                with dve.Fori(1, NOV) as i:
                    with dve.If(i < n_over):
                        gated(0, i + E)
                        take_hidden(0, i + E)
                        result(0, 1, i + E)

            for n, (a, b) in enumerate(HALVES):
                dve.wait_ge(yb_in[n], 16)
                need(mark(nc.vector.tensor_tensor(acc[:, a:b, :], h2[:, a:b, :], yb[:, a:b, 0, :], ALU.add)))
                nc.vector.tensor_tensor(fin[:, a:b, :], acc[:, a:b, :], yb[:, a:b, 1, :], ALU.add).then_inc(fin_ready, 1)

        @block.tensor
        def _(pe):
            mm = nc.tensor.matmul
            pe.wait_ge(in_first, 16)
            pe.wait_ge(in_rows, 16)
            pe.wait_ge(ones_set, 1)
            for t in range(T):
                o = ps[:, t, 0:D]
                mm(o, ones1[:, :], tokB[:, :], start=True, stop=False)
                for c in range(2):
                    a = (2 * t + c) * B
                    last = mm(o, xT[:, a:a + P], tokW[:, c, :], start=False, stop=(c == 1))
                last.then_inc(proj_ps, 1)
            pe.wait_ge(in_table, 16)
            for t in range(T):
                pe.wait_ge(xn_ready, t + 1)
                nc.tensor.transpose(ps[:, t, P:2 * P], xn[:, t, :], ident).then_inc(xnT_ps, 1)

            def values(k):
                return mm(ps[:, VALUES + k // 4, (k % 4) * D:(k % 4 + 1) * D],
                          xnT[:, k, :, :].rearrange("p r b -> p (r b)"),
                          cst[:, C_WQKV + 2 * D:C_WQKV + 3 * D], start=True, stop=True)

            for t in range(T - 1):
                pe.wait_ge(xnT_ready, t + 1)
                for k in (2 * t, 2 * t + 1):
                    values(k)
            pe.wait_ge(xnT_ready, T)
            for n, part in enumerate((1, 0)):
                w = cst[:, C_WQKV + part * D:C_WQKV + (part + 1) * D]
                mm(ps[:, 2 * n, :], w, xnT[:, 0:8, 0, :], start=True, stop=True)
                mm(ps[:, 2 * n + 1, 0:TOK - 512], w, xnT[:, 8:S, 0, :], start=True, stop=True).then_inc(qk_ps, 1)
            values(S - 2)
            values(S - 1).then_inc(v_ps, 1)

            def scores(i):
                o = ps[:, SCORES[i % 2], 0:S * H]
                pe.wait_ge(prod_ready, i + 1)
                if i == 0:
                    pe.wait_ge(bias_ready, 1)
                if i >= 2:
                    pe.wait_ge(sub_ready, i - 1)
                mm(o, cst[0:2, C_PAR:C_PAR + P], bias[:, i, :], start=True, stop=False, skip_group_check=True)
                for k in range(S):
                    last = mm(o[:, k * H:(k + 1) * H], prod[:, i, k * P:(k + 1) * P],
                              cst[:, C_HEAD:C_HEAD + H], start=False, stop=(k == S - 1), skip_group_check=True)
                last.then_inc(scores_ps, 1)

            def heads_out(i):
                pe.wait_ge(pv_ready, i + 1)
                for k in range(S):
                    last = mm(ps[:, HEADS, 0:P], prodv[:, i % 2, k * D:(k + 1) * D], ident,
                              start=(k == 0), stop=(k == S - 1))
                last.then_inc(o_ps, 1)

            def project(i):
                pe.wait_ge(oT_ready, i + 1)
                if i >= 1:
                    pe.wait_ge(var_ready, 2 + i)
                mm(ps[:, ATTN, 0:D], oT[:, i, :], outW, start=True, stop=True).then_inc(a_ps, 1)

            def logits(i):
                pe.wait_ge(x2_ready, i + 1)
                nc.tensor.transpose(ps[:, ROUTE, 0:P], pay[:, 0, i, 0:D], ident).then_inc(x2T_ps, 1)
                pe.wait_ge(x2T_ready, i + 1)
                mm(ps[:, ROUTE, P:P + E], x2T[:, i, :], routeW, start=True, stop=True).then_inc(lg_ps, 1)

            def ranks(i):
                o = ps[:, ROUTE, P + E:P + 2 * E]
                pe.wait_ge(mask_ready, i + 1)
                mm(o, cst[:, C_TRI:C_TRI + P], mask[:, i, :], start=True, stop=False)
                mm(o, cst[:, C_ONE:C_ONE + P], cum[:, i, :], start=False, stop=True).then_inc(rank_ps, 1)

            scores(0)
            for j in range(T + 2):
                if 1 <= j <= T:
                    project(j - 1)
                if j >= 2:
                    logits(j - 2)
                if j + 1 < T:
                    scores(j + 1)
                if j >= 2:
                    ranks(j - 2)
                if j < T:
                    heads_out(j)
            pe.wait_ge(slot_ready, T)
            mm(ps[:, ROUTE, P + 2 * E:P + 3 * E], cst[:, C_ONE:C_ONE + P], cum[:, T, :],
               start=True, stop=True).then_inc(cnt_ps, 1)
            pe.wait_ge(in_expert, 16 * (E // NBUF))
            pe.wait_ge(ctl_ready, 1)
            n_over = pe.value_load(ctl[0:1, 0:1], min_val=0, max_val=NOV)
            owner0 = pe.value_load(ctl[0:1, 1:2], min_val=0, max_val=E - 1)

            def rows_T(src, e, landed, count):
                pe.wait_ge(landed, count)
                nc.tensor.transpose(ps[:, ROWS_T, 0:P], xs[:, src, 0:D], ident).then_inc(xsT_ps, 1)

            def gate_up(b, e, w):
                pe.wait_ge(xsT_ready, e + 1)
                mm(ps[:, GATE[b], :], xsT[:, b, :], expW[:, bass.ds(w * WROW, 2 * F)],
                   start=True, stop=True).then_inc(g_ps, 1)

            def hidden_T(b, e):
                pe.wait_ge(hid_ready, e + 2)
                for c in range(2):
                    last = nc.tensor.transpose(ps[:, HID_T[b], c * P:(c + 1) * P],
                                               hid[:, b, c * P:(c + 1) * P], ident)
                last.then_inc(hidT_ps, 1)

            def down(b, e, w):
                pe.wait_ge(hidT_ready, e + 1)
                for c in range(2):
                    last = mm(ps[:, RESULT[b], 0:D], hidT[:, b, c, :],
                              expW[:, bass.ds(w * WROW + (2 * F + c * D), D)], start=(c == 0), stop=(c == 1))
                last.then_inc(y_ps, 1)

            def step(r, e):
                in_loop = not isinstance(e, int)
                n = r + 2
                if in_loop or e + 2 < BLK:
                    pe.wait_ge(xsT_ready, e + 2)
                    rows_T(n % NBUF, e + 2, xs_in[n % NBUF], (e - r) * (16 // NBUF) + 16 * (n // NBUF + 1))
                if in_loop or e + 1 < BLK:
                    pe.wait_ge(hid_ready, e + 1)
                    gate_up((r + 1) % 2, e + 1, e + 1 if in_loop or e + 1 < E else owner0)
                hidden_T(r % 2, e)
                if in_loop or e >= 1:
                    down((r + 1) % 2, e - 1, e - 1)

            rows_T(0, 0, xs_in[0], 16)
            gate_up(0, 0, 0)
            pe.wait_ge(xsT_ready, 1)
            rows_T(1, 1, xs_in[1], 16)
            step(0, 0)
            with pe.Fori(0, E // NBUF - 1) as g:
                for k in range(NBUF):
                    step(k + 1, g * NBUF + (k + 1))
            for e in range(E - NBUF + 1, BLK):
                step(e % NBUF, e)
            down(0, E, owner0)
            with pe.If(n_over > 1):
                with pe.Fori(1, NOV) as i:
                    with pe.If(i < n_over):
                        owner = pe.value_load(ctl[0:1, bass.ds(i + 1, 1)], min_val=0, max_val=E - 1)
                        rows_T(0, i + E, xs_over, i * 16)
                        gate_up(0, i + E, owner)
                        hidden_T(0, i + E)
                        down(0, i + E, owner)


_ARGS = ["first", "rows", "gb", "t_head", "table", "expert_w"]



def kernel(x, L0_tok_W, L0_tok_b, L0_tok_gamma, L0_tok_beta, L0_attn_in_proj_w, L0_attn_in_proj_b,
           L0_attn_out_proj_w, L0_attn_out_proj_b, L0_attn_t, L0_ffn_router_w, L0_ffn_gate_w,
           L0_ffn_up_w, L0_ffn_down_w):
    import numpy as _np
    import concourse.bacc as _bacc
    from concourse import mybir as _mybir
    from concourse.bass_utils import run_bass_kernel_spmd as _run

    a = _np.ascontiguousarray
    xf = _np.asarray(x).reshape(B, -1)[:, :CHUNKS * P]
    ex = [a(_np.asarray(L0_ffn_gate_w).transpose(1, 0, 2)),
          a(_np.asarray(L0_ffn_up_w).transpose(1, 0, 2)),
          a(_np.asarray(L0_ffn_down_w).reshape(E, 2, P, D).transpose(2, 0, 1, 3).reshape(P, E, 2 * D))]
    inb = _np.asarray(L0_attn_in_proj_b)
    x_t = xf.reshape(B, CHUNKS, P).transpose(2, 1, 0).reshape(P, CHUNKS * B)
    tok_w = _np.asarray(L0_tok_W).reshape(2, P, D).transpose(1, 0, 2).reshape(P, 2 * D)
    data = {
        "first": _np.concatenate([x_t, tok_w], axis=1),
        "rows": _np.asarray(L0_tok_b).reshape(1, D),
        "gb": _np.concatenate([_np.asarray(v) for v in (L0_tok_gamma, L0_tok_beta, L0_attn_out_proj_b)]),
        "t_head": _np.asarray(L0_attn_t),
        "table": _np.concatenate([constants(), _np.asarray(L0_attn_in_proj_w).T, _np.asarray(L0_attn_out_proj_w).T,
                                  _np.asarray(L0_ffn_router_w).T, inb.reshape(3, D).T], axis=1),
        "expert_w": _np.concatenate(ex, axis=2).reshape(P, E * WROW),
    }
    nc = _bacc.Bacc("TRN2", target_bir_lowering=False, num_devices=1)
    arrays, args = {}, []
    for name in _ARGS:
        v = a(data[name])
        arrays[name + "_dram"] = v
        args.append(nc.dram_tensor(name + "_dram", v.shape, _mybir.dt.from_np(v.dtype), kind="ExternalInput").ap())
    out = nc.dram_tensor("out_dram", (B, S, D), _mybir.dt.float32, kind="ExternalOutput").ap()
    audio_tower(nc, *args, out)
    r = _run(nc, [arrays], core_ids=[0])
    return r.results[0]["out_dram"]
```

```python
from contextlib import ExitStack

import numpy as np

import concourse.bass as bass
from concourse import mybir

F32 = mybir.dt.float32
U32 = mybir.dt.uint32
I32 = mybir.dt.int32
ALU = mybir.AluOpType
ACT = mybir.ActivationFunctionType
AX_X = mybir.AxisListType.X

P = 128
B = 64
S = 10
T = S // 2
D = 128
H = 8
DH = D // H
E = 16
F = 256
TOPK = 2
TOK = B * S
CHUNKS = S + 1
WROW = 2 * F + F
MAXB = TOK // P
NOV = (TOK * TOPK - E) // P
BLK = E + 1
ROWS = E * TOK
ROW = D + 2
NBUF = 4
FILL = 10
EPS_TOK = 1e-3
EPS_LN = 1e-5
FAR = -1e30

C_ID = 0
C_TRI = C_ID + P
C_ONE = C_TRI + P
C_HEAD = C_ONE + P
C_IOTA = C_HEAD + (2 * S - 1) * H
C_EBASE = C_IOTA + E
C_PAR = C_EBASE + E
C_DIST = C_PAR + P
C_HALF = C_DIST + T * S
C_THR = C_HALF + T
C_BLK = C_THR + MAXB - 1
C_DST = C_BLK + NOV
C_WQKV = C_DST + TOPK * T
C_WOUT = C_WQKV + 3 * D
C_WROUTE = C_WOUT + D
C_BQKV = C_WROUTE + E
C_END = C_BQKV + 3


def constants():
    p = np.arange(P)
    c = np.zeros((P, C_WQKV), np.float32)
    c[:, C_ID:C_ID + P] = np.eye(P)
    c[:, C_TRI:C_TRI + P] = p[:, None] < p[None, :]
    c[:, C_ONE:C_ONE + P] = 1.0
    c[:, C_HEAD + (S - 1) * H:C_HEAD + S * H] = (p[:, None] // DH == np.arange(H)[None, :]) * DH ** -0.5
    c[:, C_IOTA:C_IOTA + E] = np.arange(E)
    c[0, C_EBASE:C_EBASE + E] = np.arange(E) * TOK
    c[0:2, C_PAR:C_PAR + P] = np.arange(2)[:, None] == p[None, :] // B
    q = 2 * np.arange(T)[None, :, None] + np.arange(2)[:, None, None]
    c[0:2, C_DIST:C_DIST + T * S] = (-(q - np.arange(S)[None, None, :]) ** 2.0).reshape(2, T * S)
    c[:, C_HALF:C_HALF + T] = -0.5
    c[:, C_THR:C_THR + MAXB - 1] = P * np.arange(1, MAXB)
    c[:, C_BLK:C_BLK + NOV] = np.arange(NOV)
    dst = P * (TOPK * np.arange(T)[None, :] + np.arange(TOPK)[:, None])
    c[:, C_DST:C_WQKV] = dst.reshape(1, -1) + p[:, None]
    return c


def audio_tower(nc, first, rows_d, gb, t_head, table, expert_w, out):
    with ExitStack() as ctx:
        def sb(name, shape, dt=F32):
            return ctx.enter_context(nc.sbuf_tensor(name, shape, dt))

        def sem(name):
            return ctx.enter_context(nc.semaphore(name))

        ps = ctx.enter_context(nc.psum_tensor("ps", [P, 8, 512], F32))

        xw = sb("xw", [P, CHUNKS * B + 2 * D])
        xT = xw[:, 0:CHUNKS * B]
        tokW = xw[:, CHUNKS * B:].rearrange("p (c d) -> p c d", c=2)
        tokB = sb("tokB", [P, D])
        ones = sb("ones", [P, P])
        zeros = sb("zeros", [P, P])
        gbo = sb("gbo", [P, 3, D])
        headT = sb("headT", [2, H])
        cst = sb("cst", [P, C_END])
        expW = sb("expW", [P, E * WROW])

        stats = sb("stats", [P, T, 6])
        mv = sb("mv", [P, T, 2])
        mve = sb("mve", [P, T])
        rstd = sb("rstd", [P, T])
        nmr = sb("nmr", [P, T])
        pg = sb("pg", [P, T, D])
        h = sb("h", [P, T, D])
        hb = sb("hb", [P, T, D])
        xn = sb("xn", [P, T, D])
        xnT = sb("xnT", [P, S, 2, B])
        qT = sb("qT", [P, TOK])
        kT = sb("kT", [P, TOK])
        actw = sb("actw", [1, 1])
        sig = sb("sig", [2, 4, H])
        bias = sb("bias", [2, T, S * H])
        prod = sb("prod", [P, T, S * P])
        sT = sb("sT", [S * H, T, P])
        mx = sb("mx", [P, 2, H])
        sc = sb("sc", [P, 2, S * H])
        ex = sb("ex", [P, 2, S * H])
        den = sb("den", [P, 2, H])
        rden = sb("rden", [P, 2, H])
        pn = sb("pn", [P, 2, S * H])
        v = sb("v", [P, S * D])
        prodv = sb("prodv", [P, 2, S * D])
        osum = sb("osum", [P, 2, D])
        oT = sb("oT", [P, T, P])
        h2 = sb("h2", [P, T, D])
        pay = sb("pay", [P, TOPK, T, ROW])
        x2T = sb("x2T", [P, T, P])
        top = sb("top", [P, T, 8])
        topi = sb("topi", [P, T, 8], U32)
        idxf = sb("idxf", [P, T, TOPK])
        oh = sb("oh", [P, T, TOPK, E])
        mask = sb("mask", [P, T, E])
        cum = sb("cum", [P, T, E])
        chosen = sb("chosen", [1, E])
        ed = sb("ed", [P, T])
        ed1 = sb("ed1", [P, T])
        spick = sb("spick", [P, T, TOPK, E])
        slotf = sb("slotf", [P, T, TOPK])
        slot = sb("slot", [P, T, TOPK], U32)
        ovm = sb("ovm", [1, E, MAXB - 1])
        nov = sb("nov", [1, E])
        novi = sb("novi", [1, E])
        eom = sb("eom", [1, NOV, E])
        eov = sb("eov", [1, NOV, E])
        eof = sb("eof", [1, NOV])
        eof2 = sb("eof2", [1, NOV])
        eob = sb("eob", [1, NOV])
        eor = sb("eor", [1, NOV])
        eor2 = sb("eor2", [1, NOV])
        ctl = sb("ctl", [1, 1 + 2 * NOV], I32)
        blank = sb("blank", [P, FILL, ROW])
        xs = sb("xs", [P, NBUF, ROW])
        meta = sb("meta", [P, BLK + NOV, 2])
        xsT = sb("xsT", [P, NBUF, P])
        sg = sb("sg", [P, NBUF, F])
        hid = sb("hid", [P, 2, F])
        hidT = sb("hidT", [P, 2, 2, P])
        ys = sb("ys", [P, NBUF, D])
        yi = sb("yi", [P, NBUF], U32)
        yb = sb("yb", [P, TOPK, T, D])
        acc = sb("acc", [P, T, D])
        fin = sb("fin", [P, T, D])

        disp = nc.dram_tensor("disp", [ROWS, ROW], F32).ap()
        ybuf = nc.dram_tensor("ybuf", [TOPK * TOK, D], F32).ap()

        in_first = sem("in_first")
        in_rows = sem("in_rows")
        in_ln = sem("in_ln")
        in_head = sem("in_head")
        in_table = sem("in_table")
        in_expert = sem("in_expert")
        tokB_clear = sem("tokB_clear")
        zeros_set = sem("zeros_set")
        ones_set = sem("ones_set")
        s_blank = sem("s_blank")
        s_filled = sem("s_filled")
        dv = sem("dv")
        var_ready = sem("var_ready")
        rstd_ready = sem("rstd_ready")
        proj_ps = sem("proj_ps")
        h_ready = sem("h_ready")
        hb_ready = sem("hb_ready")
        xn_ready = sem("xn_ready")
        xnT_ps = sem("xnT_ps")
        xnT_even = sem("xnT_even")
        xnT_odd = sem("xnT_odd")
        qk_ps = sem("qk_ps")
        k_ready = sem("k_ready")
        q_ready = sem("q_ready")
        v_ps = sem("v_ps")
        v_ready = sem("v_ready")
        bias_ready = sem("bias_ready")
        prod_first = sem("prod_first")
        prod_ready = sem("prod_ready")
        sT_ps = sem("sT_ps")
        sT_ready = sem("sT_ready")
        scores_ps = sem("scores_ps")
        sub_ready = sem("sub_ready")
        exp_ready = sem("exp_ready")
        pn_ready = sem("pn_ready")
        pv_ready = sem("pv_ready")
        osum_ready = sem("osum_ready")
        o_ps = sem("o_ps")
        oT_ready = sem("oT_ready")
        a_ps = sem("a_ps")
        pl = sem("pl")
        stats_ready = sem("stats_ready")
        nmr_ready = sem("nmr_ready")
        x2_ready = sem("x2_ready")
        h2_ready = sem("h2_ready")
        x2T_ps = sem("x2T_ps")
        x2T_ready = sem("x2T_ready")
        lg_ps = sem("lg_ps")
        top_ready = sem("top_ready")
        ed_ready = sem("ed_ready")
        mask_ready = sem("mask_ready")
        rank_ps = sem("rank_ps")
        cnt_ps = sem("cnt_ps")
        slot_ready = sem("slot_ready")
        ctl_ready = sem("ctl_ready")
        s_disp = sem("s_disp")
        xs_in = [sem(f"xs_in{u}") for u in range(NBUF)]
        xs_over = sem("xs_over")
        xs_used = sem("xs_used")
        xsT_ps = sem("xsT_ps")
        xsT_ready = sem("xsT_ready")
        g_ps = sem("g_ps")
        sg_ready = sem("sg_ready")
        hid_ready = sem("hid_ready")
        hidT_ps = sem("hidT_ps")
        hidT_ready = sem("hidT_ready")
        y_ps = sem("y_ps")
        y_ready = sem("y_ready")
        y_taken = sem("y_taken")
        y_out = [sem(f"y_out{u}") for u in range(NBUF)]
        y_over = sem("y_over")
        over_done = sem("over_done")
        yb_in = [sem(f"yb_in{n}") for n in range(2)]
        fin_ready = sem("fin_ready")
        s_out = sem("s_out")

        ident = cst[:, C_ID:C_ID + P]
        outW = cst[:, C_WOUT:C_WOUT + D]
        routeW = cst[:, C_WROUTE:C_WROUTE + E]

        SCORES = (0, 4, 5, 6, 7)
        HEADS, ROUTE = 1, 2
        VALUES = 5
        IDLE = 7
        FREED = 3
        SENT = (0, 1, 2, 4, 8, TOPK * T)
        EARLY = 2
        GATE, ROWS_T, HID_T, RESULT = (0, 1, 3, 4), 5, 6, (7, 2)
        FIRST_ROWS = (5, 6, 7)
        HALVES = ((0, 3), (3, T))

        def products(engine, i, a=0, b=S):
            return engine.tensor_tensor(
                prod[:, i, a * P:b * P].rearrange("p (k r b) -> p k r b", k=b - a, r=2),
                qT[:, i * P:(i + 1) * P].rearrange("p (r b) -> p r b", r=2).unsqueeze(1)
                .broadcast_to([P, b - a, 2, B]),
                kT[:, a * B:b * B].rearrange("p (k b) -> p k b", k=b - a).unsqueeze(2)
                .broadcast_to([P, b - a, 2, B]), ALU.mult)

        def filled(t):
            return cst[:, C_EBASE:C_EBASE + E] if t == 0 else cum[:, t - 1, :]

        def weighted_values(engine, i):
            return engine.tensor_tensor(
                prodv[:, i % 2, :].rearrange("p (n d) -> p n d", d=DH),
                v[:, :].rearrange("p (n d) -> p n d", d=DH),
                pn[:, i % 2, :].unsqueeze(2).broadcast_to([P, S * H, DH]), ALU.mult)

        def twice(t):
            return (xnT[:, 2 * t:2 * t + 2, :, :],
                    ps[:, t, P:2 * P].rearrange("p (r b) -> p r b", r=2).unsqueeze(2).broadcast_to([P, 2, 2, B]))

        def stream_ps(t):
            return ps[:, SCORES[t], 3 * P:3 * P + D]

        block = ctx.enter_context(nc.Block())

        @block.sync
        def _(sp):
            sp.dma_start(xw[:, :], first).then_inc(in_first, 16)
            sp.dma_start(headT[:, :], t_head.partition_broadcast(2)).then_inc(in_head, 16)
            sp.wait_ge(s_blank, 2)
            sp.wait_ge(in_table, 16)
            sp.dma_start(disp.rearrange("(p n r) c -> p n (r c)", p=P, r=FILL),
                         blank[:, :, :].rearrange("p r c -> p (r c)").unsqueeze(1)
                         .broadcast_to([P, ROWS // P // FILL, FILL * ROW])).then_inc(s_filled, 16)
            for g in range(0, E, NBUF):
                sp.dma_start(expW[:, g * WROW:(g + NBUF) * WROW],
                             expert_w[:, g * WROW:(g + NBUF) * WROW]).then_inc(in_expert, 16)

            sp.wait_ge(s_disp, 16 * T * TOPK)
            for u in range(NBUF):
                sp.dma_start(xs[:, u, :], disp[u * TOK:u * TOK + P, :]).then_inc(xs_in[u], 16)
            with sp.Fori(1, E // NBUF) as g:
                for u in range(NBUF):
                    row = sp.snap((g * NBUF + u) * TOK)
                    sp.wait_ge(xs_used, g * NBUF + (u - NBUF + 1))
                    sp.dma_start(xs[:, u, :], disp[bass.ds(row, P), :]).then_inc(xs_in[u], 16)
            sp.wait_ge(ctl_ready, 1)
            n_over = sp.value_load(ctl[0:1, 0:1], min_val=0, max_val=NOV)
            row = sp.value_load(ctl[0:1, 1 + NOV:2 + NOV], min_val=0, max_val=ROWS // P - 1) * P
            sp.wait_ge(xs_used, E - NBUF + 1)
            sp.dma_start(xs[:, 0, :], disp[bass.ds(row, P), :]).then_inc(xs_in[0], 16)
            with sp.If(n_over > 1):
                with sp.Fori(1, NOV) as i:
                    with sp.If(i < n_over):
                        row = sp.snap(sp.value_load(ctl[0:1, bass.ds(i + (1 + NOV), 1)],
                                                    min_val=0, max_val=ROWS // P - 1) * P)
                        sp.wait_ge(y_ready, i + E)
                        sp.dma_start(xs[:, 0, :], disp[bass.ds(row, P), :]).then_inc(xs_over, 16)
                        sp.wait_ge(y_over, i * 16)
                        sp.sem_inc(over_done, 1)

            for u in range(NBUF):
                sp.wait_ge(y_out[u], 16 * (E // NBUF + (u == 0)))
            yv = ybuf.rearrange("(t j p) c -> j p t c", j=TOPK, p=P)
            for n in range(TOPK):
                sp.dma_start(yb[:, n, :, :], yv[n]).then_inc(yb_in[n], 16)
            sp.wait_ge(fin_ready, 1)
            sp.dma_start(out.rearrange("b (t r) d -> r b t d", r=2)[0], fin[0:B, :, :]).then_inc(s_out, 16)
            sp.wait_ge(s_out, 16 * 2)

        @block.gpsimd
        def _(pool):
            nc.gpsimd.memset(blank[:, :, :], 0.0).then_inc(s_blank, 1)
            pool.wait_ge(s_blank, 1)
            nc.gpsimd.memset(blank[:, :, D:D + 1], float(4 * TOPK * TOK)).then_inc(s_blank, 1)
            pool.wait_ge(in_table, 16)

            def power(n, a, b):
                pool.wait_ge(var_ready, n)
                nc.gpsimd.tensor_tensor(rstd[:, a:b], mve[:, a:b], cst[:, C_HALF + a:C_HALF + b],
                                        ALU.pow).then_inc(rstd_ready, 1)

            for n in range(4):
                power(1 + n, *HALVES[n % 2])
            pool.wait_ge(in_ln, 16)
            pool.wait_ge(h_ready, 2)
            nc.gpsimd.tensor_tensor(hb[:, :, :], h[:, :, :], gbo[:, 2, :].unsqueeze(1).broadcast_to([P, T, D]),
                                    ALU.add).then_inc(hb_ready, 1)

            pool.wait_ge(k_ready, 1)
            pool.wait_ge(q_ready, 1)
            for i in range(EARLY, T):
                products(nc.gpsimd, i).then_inc(prod_ready, 1)

            def weigh(i):
                pool.wait_ge(v_ready, 1)
                pool.wait_ge(pn_ready, i + 1)
                weighted_values(nc.gpsimd, i).then_inc(pv_ready, 1)

            def dispatch(t, j):
                if t == 0 and j == 0:
                    pool.wait_ge(s_filled, 16)
                pool.wait_ge(slot_ready, t + 1)
                pool.wait_ge(x2_ready, TOPK * t + j + 1)
                nc.gpsimd.indirect_dma_start(
                    out=disp, out_offset=bass.IndirectOffsetOnAxis(ap=slot[:, t, j:j + 1], axis=0),
                    in_=pay[:, j, t, :], in_offset=None).then_inc(s_disp, 16)

            def scale_and_shift(t):
                pool.wait_ge(stats_ready, t + 1)
                nc.gpsimd.tensor_scalar(mve[:, t:t + 1], mv[:, t, 1:2], EPS_LN, None, ALU.add).then_inc(pl, 1)
                pool.wait_ge(pl, 3 * t + 1)
                nc.gpsimd.tensor_tensor(rstd[:, t:t + 1], mve[:, t:t + 1], cst[:, C_HALF + t:C_HALF + t + 1],
                                        ALU.pow).then_inc(pl, 1)
                pool.wait_ge(pl, 3 * t + 2)
                nc.gpsimd.tensor_scalar(nmr[:, t:t + 1], mv[:, t, 0:1], rstd[:, t:t + 1], -1.0,
                                        ALU.mult, ALU.mult).then_inc(pl, 1)
                pool.wait_ge(pl, 3 * t + 3)
                pool.sem_inc(nmr_ready, 1)

            weigh(1)
            sent = 0
            for j in range(T + 1):
                if j < T:
                    scale_and_shift(j)
                if j + 2 < T:
                    weigh(j + 2)
                for n in range(sent, SENT[j]):
                    dispatch(n // TOPK, n % TOPK)
                sent = SENT[j]

            def scatter(u, done):
                nc.gpsimd.indirect_dma_start(
                    out=ybuf, out_offset=bass.IndirectOffsetOnAxis(ap=yi[:, u:u + 1], axis=0),
                    in_=ys[:, u, :], in_offset=None, bounds_check=TOPK * TOK - 1,
                    oob_is_err=False).then_inc(done, 16)

            with pool.Fori(0, E // NBUF) as g:
                for u in range(NBUF):
                    pool.wait_ge(y_ready, g * NBUF + (u + 1))
                    pool.sem_inc(y_taken, 1)
                    scatter(u, y_out[u])
            pool.wait_ge(y_ready, BLK)
            scatter(0, y_out[0])
            n_over = pool.value_load(ctl[0:1, 0:1], min_val=0, max_val=NOV)
            with pool.If(n_over > 1):
                with pool.Fori(1, NOV) as i:
                    with pool.If(i < n_over):
                        pool.wait_ge(y_ready, i + BLK)
                        pool.sem_inc(y_taken, 1)
                        scatter(1, y_over)

        @block.scalar
        def _(act):
            act.wait_ge(tokB_clear, 1)
            act.dma_start(tokB[0:1, :], rows_d).then_inc(in_rows, 16)
            act.dma_start(gbo[:, :, :].rearrange("p a d -> p (a d)"), gb.partition_broadcast(P)).then_inc(in_ln, 16)
            act.dma_start(cst[:, :], table).then_inc(in_table, 16)
            act.wait_ge(ones_set, 1)
            nc.scalar.activation(actw[:, :], ones[0:1, 0:1], ACT.Exp)
            act.wait_ge(in_table, 16)
            for t in range(0, T, 2):
                act.wait_ge(xnT_ps, t + 1)
                nc.scalar.copy(*twice(t)).then_inc(xnT_even, 1)
            act.wait_ge(qk_ps, 1)
            nc.scalar.activation(kT[:, :], ps[:, 0:2, :].rearrange("p a b -> p (a b)")[:, 0:TOK],
                                 ACT.Identity, bias=cst[:, C_BQKV + 1:C_BQKV + 2]).then_inc(k_ready, 1)

            act.wait_ge(v_ps, 1)
            nc.scalar.copy(v[:, :], ps[:, VALUES:VALUES + 3, :].rearrange("p a b -> p (a b)")[:, 0:S * D]
                           ).then_inc(v_ready, 1)

            def exponent(i):
                act.wait_ge(sub_ready, i + 1)
                nc.scalar.activation(ex[:, i % 2, :], sc[:, i % 2, :], ACT.Exp).then_inc(exp_ready, 1)

            def take_scores(i):
                act.wait_ge(sT_ps, i + 1)
                nc.scalar.copy(sT[:, i, :], ps[0:S * H, SCORES[i], P:2 * P]).then_inc(sT_ready, 1)

            def normalised(t, n):
                act.wait_ge(nmr_ready, t + 1)
                nc.scalar.activation(pay[:, n, t, 0:D], stream_ps(t), ACT.Identity,
                                     bias=nmr[:, t:t + 1], scale=rstd[:, t:t + 1]).then_inc(x2_ready, 1)

            for i in range(2):
                take_scores(i)
                exponent(i)
            take_scores(2)
            for j in range(T + 1):
                t = j - 1
                if j >= 1:
                    normalised(t, 0)
                    nc.scalar.copy(h2[:, t, :], stream_ps(t)).then_inc(h2_ready, 1)
                if j == 2:
                    exponent(4)
                if j < T:
                    act.wait_ge(o_ps, j + 1)
                    nc.scalar.activation(oT[:, j, :], ps[:, HEADS, 0:P], ACT.Identity,
                                         bias=cst[:, C_BQKV + 2:C_BQKV + 3]).then_inc(oT_ready, 1)
                if j == 1:
                    exponent(3)
                if j >= 1:
                    act.wait_ge(x2T_ps, t + 1)
                    nc.scalar.copy(x2T[:, t, :], ps[:, ROUTE, 0:P]).then_inc(x2T_ready, 1)
                    normalised(t, 1)
                if j == 0:
                    exponent(2)
                if j + 3 < T:
                    take_scores(j + 3)
                if j >= 1:
                    act.wait_ge(top_ready, t + 1)
                    nc.scalar.activation(ed[:, t:t + 1], top[:, t, 0:1], ACT.Exp, bias=top[:, t, 1:2],
                                         scale=-1.0).then_inc(ed_ready, 1)
            nc.scalar.activation(actw[:, :], ones[0:1, 0:1], ACT.Silu)

            def take_rows(b, src, e, bank=ROWS_T):
                act.wait_ge(xsT_ps, e + 1)
                nc.scalar.copy(xsT[:, b, :], ps[:, bank, 0:P]).then_inc(xsT_ready, 1)
                nc.scalar.copy(meta[:, bass.ds(e, 1), :].rearrange("p a c -> p (a c)"),
                               xs[:, src, D:ROW]).then_inc(xs_used, 1)

            def silu(b, e):
                act.wait_ge(g_ps, e + 1)
                nc.scalar.activation(sg[:, b, :], ps[:, GATE[b], 0:F], ACT.Silu).then_inc(sg_ready, 1)

            AHEAD = 3
            for e in range(AHEAD):
                take_rows(e, e, e, FIRST_ROWS[e])
            with act.Fori(0, E // NBUF - 1) as g:
                for u in range(NBUF):
                    silu(u, g * NBUF + u)
                    take_rows((u + AHEAD) % NBUF, (u + AHEAD) % NBUF, g * NBUF + (u + AHEAD))
            for e in range(E - NBUF, BLK):
                silu(e % NBUF, e)
                if e + AHEAD < BLK:
                    take_rows((e + AHEAD) % NBUF, (e + AHEAD) % NBUF, e + AHEAD)
            n_over = act.value_load(ctl[0:1, 0:1], min_val=0, max_val=NOV)
            with act.If(n_over > 1):
                with act.Fori(1, NOV) as i:
                    with act.If(i < n_over):
                        take_rows(0, 0, i + E)
                        silu(0, i + E)
            act.wait_ge(fin_ready, 1)
            act.dma_start(out.rearrange("b (t r) d -> r b t d", r=2)[1], fin[B:P, :, :]).then_inc(s_out, 16)

        @block.vector
        def _(dve):
            count = [0]

            def mark(ins):
                count[0] += 1
                ins.then_inc(dv, 1)
                return count[0]

            def need(step):
                dve.wait_ge(dv, step)

            nc.vector.memset(tokB[:, :], 0.0).then_inc(tokB_clear, 1)
            nc.vector.memset(zeros[:, :], 0.0).then_inc(zeros_set, 1)
            nc.vector.memset(ones[:, :], 1.0).then_inc(ones_set, 1)
            nc.vector.memset(ctl[:, :], 0).then_inc(hid_ready, 1)
            dve.wait_ge(in_ln, 16)
            def centre(n, a, b):
                for t in range(a, b):
                    dve.wait_ge(proj_ps, t + 1)
                    got = mark(nc.vector.bn_stats(stats[:, t, :], ps[:, t, 0:D]))
                    if t > a:
                        need(aggregated)
                        mark(nc.vector.scalar_tensor_tensor(pg[:, t - 1, :], ps[:, t - 1, 0:D], mv[:, t - 1, 0:1],
                                                            gbo[:, 0, :], ALU.subtract, ALU.mult))
                    need(got)
                    aggregated = mark(nc.vector.bn_aggr(mv[:, t, :], stats[:, t, :]))
                need(aggregated)
                nc.vector.tensor_scalar(mve[:, a:b], mv[:, a:b, 1], EPS_TOK, None, ALU.add).then_inc(var_ready, 1)
                return mark(nc.vector.scalar_tensor_tensor(pg[:, b - 1, :], ps[:, b - 1, 0:D], mv[:, b - 1, 0:1],
                                                           gbo[:, 0, :], ALU.subtract, ALU.mult))

            def scale(n, a, b, centred):
                dve.wait_ge(rstd_ready, n)
                need(centred)
                for t in range(a, b):
                    got = mark(nc.vector.scalar_tensor_tensor(h[:, t, :], pg[:, t, :], rstd[:, t:t + 1],
                                                              gbo[:, 1, :], ALU.mult, ALU.add))
                need(got)
                nc.vector.sem_inc(h_ready, 1)
                for t in range(a, b):
                    got = mark(nc.vector.bn_stats(stats[:, t, :], h[:, t, :]))
                need(got)
                for t in range(a, b):
                    got = mark(nc.vector.bn_aggr(mv[:, t, :], stats[:, t, :]))
                need(got)
                nc.vector.tensor_scalar(mve[:, a:b], mv[:, a:b, 1], EPS_LN, None, ALU.add).then_inc(var_ready, 1)

            def normal(n, a, b):
                dve.wait_ge(rstd_ready, n)
                for t in range(a, b):
                    nc.vector.tensor_scalar(xn[:, t, :], h[:, t, :], mv[:, t, 0:1], rstd[:, t:t + 1],
                                            ALU.subtract, ALU.mult).then_inc(xn_ready, 1)

            (a0, b0), (a1, b1) = HALVES
            c0 = centre(1, a0, b0)
            c1 = centre(2, a1, b1)
            scale(1, a0, b0, c0)
            scale(2, a1, b1, c1)
            normal(3, a0, b0)
            normal(4, a1, b1)

            for t in range(1, T, 2):
                dve.wait_ge(xnT_ps, t + 1)
                nc.vector.tensor_copy(*twice(t)).then_inc(xnT_odd, 1)
            dve.wait_ge(in_head, 16)
            need(mark(nc.vector.tensor_tensor(sig[:, 0, :], headT[:, :], headT[:, :], ALU.mult)))
            need(mark(nc.vector.scalar_tensor_tensor(sig[:, 1, :], sig[:, 0, :], 2.0, sig[:, 0, :],
                                                     ALU.mult, ALU.mult)))
            need(mark(nc.vector.tensor_scalar(sig[:, 2, :], sig[:, 1, :], 1e-37, None, ALU.max)))
            need(mark(nc.vector.reciprocal(sig[:, 3, :], sig[:, 2, :])))
            dve.wait_ge(in_table, 16)
            need(mark(nc.vector.tensor_tensor(
                bias[:, :, :].rearrange("r t (k h) -> r (t k) h", h=H),
                cst[0:2, C_DIST:C_DIST + T * S].unsqueeze(2).broadcast_to([2, T * S, H]),
                sig[:, 3, :].unsqueeze(1).broadcast_to([2, T * S, H]), ALU.mult)))
            nc.vector.tensor_scalar(bias[:, :, :], bias[:, :, :], FAR, None, ALU.max).then_inc(bias_ready, 1)
            nc.vector.tensor_copy(pay[:, :, :, D], cst[:, C_DST:C_WQKV].rearrange("p (j t) -> p j t", j=TOPK))

            dve.wait_ge(qk_ps, 2)
            nc.vector.tensor_scalar(qT[:, :], ps[:, 2:4, :].rearrange("p a b -> p (a b)")[:, 0:TOK],
                                    cst[:, C_BQKV:C_BQKV + 1], None, ALU.add).then_inc(q_ready, 1)
            dve.wait_ge(k_ready, 1)
            dve.wait_ge(q_ready, 1)
            for i in range(EARLY):
                for a in range(0, S, S // 2):
                    products(nc.vector, i, a, a + S // 2).then_inc(prod_first, 1)

            def minus_max(i):
                b = i % 2
                dve.wait_ge(scores_ps, i + 1)
                s = ps[:, SCORES[i], 0:S * H].rearrange("p (k h) -> p k h", h=H)
                need(mark(nc.vector.tensor_reduce(mx[:, b, :], s.rearrange("p k h -> p h k"), AX_X, ALU.max)))
                nc.vector.tensor_tensor(
                    sc[:, b, :].rearrange("p (k h) -> p k h", h=H), s,
                    mx[:, b, :].unsqueeze(1).broadcast_to([P, S, H]), ALU.subtract).then_inc(sub_ready, 1)

            def stream_stats(t):
                dve.wait_ge(a_ps, t + 1)
                need(mark(nc.vector.bn_stats(stats[:, t, :], stream_ps(t))))
                nc.vector.bn_aggr(mv[:, t, :], stats[:, t, :]).then_inc(stats_ready, 1)

            def softmax_and_slots(i, t):
                soft, place = i < T, t >= 0
                if place:
                    dve.wait_ge(ed_ready, t + 1)
                    one = mark(nc.vector.tensor_scalar(ed1[:, t:t + 1], ed[:, t:t + 1], 1.0, None, ALU.add))
                if soft:
                    b = i % 2
                    dve.wait_ge(exp_ready, i + 1)
                    total = mark(nc.vector.tensor_reduce(den[:, b, :], ex[:, b, :].rearrange("p (k h) -> p h k", h=H),
                                                         AX_X, ALU.add))
                if place:
                    need(one)
                    best = mark(nc.vector.reciprocal(pay[:, 0, t, D + 1:ROW], ed1[:, t:t + 1]))
                    dve.wait_ge(rank_ps, t + 1)
                    picked = mark(nc.vector.tensor_tensor(
                        spick[:, t, :, :], oh[:, t, :, :],
                        ps[:, SCORES[t], 2 * P:2 * P + E].unsqueeze(1).broadcast_to([P, TOPK, E]), ALU.mult))
                if soft:
                    need(total)
                    inverse = mark(nc.vector.reciprocal(rden[:, b, :], den[:, b, :]))
                if place:
                    need(best)
                    mark(nc.vector.tensor_tensor(pay[:, 1, t, D + 1:ROW], ed[:, t:t + 1], pay[:, 0, t, D + 1:ROW],
                                                 ALU.mult))
                    need(picked)
                    row = mark(nc.vector.tensor_reduce(slotf[:, t, :], spick[:, t, :, :], AX_X, ALU.add))
                if soft:
                    need(inverse)
                    nc.vector.tensor_tensor(
                        pn[:, b, :].rearrange("p (k h) -> p k h", h=H),
                        ex[:, b, :].rearrange("p (k h) -> p k h", h=H),
                        rden[:, b, :].unsqueeze(1).broadcast_to([P, S, H]), ALU.mult).then_inc(pn_ready, 1)
                if place:
                    mark(nc.vector.tensor_tensor(cum[:, t, :], filled(t), mask[:, t, :], ALU.add))
                    need(row)
                    nc.vector.tensor_copy(slot[:, t, :], slotf[:, t, :]).then_inc(slot_ready, 1)

            def weigh(i):
                dve.wait_ge(v_ready, 1)
                dve.wait_ge(pn_ready, i + 1)
                return mark(weighted_values(nc.vector, i))

            def sum_keys(i):
                nc.vector.tensor_reduce(osum[:, i % 2, :], prodv[:, i % 2, :].rearrange("p (k c) -> p c k", k=S),
                                        AX_X, ALU.add).then_inc(osum_ready, 1)

            def route(i):
                dve.wait_ge(lg_ps, i + 1)
                lg = ps[:, ROUTE, P:P + E]
                nc.vector.max(top[:, i, :], lg).then_inc(top_ready, 1)
                dve.wait_ge(top_ready, i + 1)
                need(mark(nc.vector.max_index(topi[:, i, :], top[:, i, :], lg)))
                need(mark(nc.vector.tensor_copy(idxf[:, i, :], topi[:, i, 0:TOPK])))
                need(mark(nc.vector.tensor_tensor(
                    oh[:, i, :, :], cst[:, C_IOTA:C_IOTA + E].unsqueeze(1).broadcast_to([P, TOPK, E]),
                    idxf[:, i, :].unsqueeze(2).broadcast_to([P, TOPK, E]), ALU.is_equal)))
                nc.vector.tensor_tensor(mask[:, i, :], oh[:, i, 0, :], oh[:, i, 1, :], ALU.add).then_inc(mask_ready, 1)

            minus_max(0)
            softmax_and_slots(0, -1)
            weighted = weigh(0)
            minus_max(1)
            for j in range(T + 2):
                if j < T:
                    if j == 0:
                        need(weighted)
                    else:
                        dve.wait_ge(pv_ready, j)
                    sum_keys(j)
                if j == 1:
                    minus_max(3)
                if j == 0:
                    softmax_and_slots(1, -1)
                    minus_max(2)
                else:
                    softmax_and_slots(j + 2, j - 2)
                if j < T:
                    stream_stats(j)
                if j == 0:
                    softmax_and_slots(2, -1)
                if 1 <= j <= T:
                    route(j - 1)
                if j >= 1 and j + 3 < T:
                    minus_max(j + 3)

            dve.wait_ge(cnt_ps, 1)
            cnt = ps[0:1, ROUTE, P + 2 * E:P + 3 * E]
            need(mark(nc.vector.tensor_tensor(chosen[:, :], cnt, cst[0:1, C_EBASE:C_EBASE + E], ALU.subtract)))
            need(mark(nc.vector.tensor_tensor(ovm[:, :, :], chosen[:, :].unsqueeze(2).broadcast_to([1, E, MAXB - 1]),
                                              cst[0:1, C_THR:C_BLK].unsqueeze(1).broadcast_to([1, E, MAXB - 1]),
                                              ALU.is_gt)))
            need(mark(nc.vector.tensor_reduce(nov[:, :], ovm[:, :, :], AX_X, ALU.add)))
            need(mark(nc.vector.tensor_tensor_scan(novi[:, :], cst[0:1, C_ONE:C_ONE + E], nov[:, :], 0.0,
                                                   ALU.mult, ALU.add)))
            mark(nc.vector.tensor_copy(ctl[0:1, 0:1], novi[0:1, E - 1:E]))
            need(mark(nc.vector.tensor_tensor(
                eom[:, :, :], novi[0:1, :].unsqueeze(1).broadcast_to([1, NOV, E]),
                cst[0:1, C_BLK:C_BLK + NOV].unsqueeze(2).broadcast_to([1, NOV, E]), ALU.is_le)))
            mark(nc.vector.tensor_tensor(eov[:, :, :], eom[:, :, :], nov[0:1, :].unsqueeze(1)
                                         .broadcast_to([1, NOV, E]), ALU.mult))
            need(mark(nc.vector.tensor_reduce(eof[:, :], eom[:, :, :], AX_X, ALU.add)))
            mark(nc.vector.tensor_reduce(eob[:, :], eov[:, :, :], AX_X, ALU.add))
            need(mark(nc.vector.tensor_scalar(eof2[:, :], eof[:, :], float(E - 1), None, ALU.min)))
            mark(nc.vector.tensor_copy(ctl[0:1, 1:1 + NOV], eof2[:, :]))
            need(mark(nc.vector.scalar_tensor_tensor(eor[:, :], eof2[:, :], float(MAXB), cst[0:1, C_BLK:C_BLK + NOV],
                                                     ALU.mult, ALU.add)))
            need(mark(nc.vector.tensor_tensor(eor2[:, :], eor[:, :], eob[:, :], ALU.subtract)))
            need(mark(nc.vector.tensor_scalar(eor[:, :], eor2[:, :], 1.0, float(ROWS // P - 1), ALU.add, ALU.min)))
            need(mark(nc.vector.tensor_copy(ctl[0:1, 1 + NOV:], eor[:, :])))
            nc.vector.sem_inc(ctl_ready, 1)

            def gated(b, e):
                dve.wait_ge(sg_ready, e + 1)
                nc.vector.tensor_tensor(hid[:, b % 2, :], sg[:, b, :], ps[:, GATE[b], F:2 * F],
                                        ALU.mult).then_inc(hid_ready, 1)

            def take_hidden(b, e):
                dve.wait_ge(hidT_ps, e + 1)
                nc.vector.tensor_copy(hidT[:, b, :, :].rearrange("p c s -> p (c s)"),
                                      ps[:, HID_T, 0:F]).then_inc(hidT_ready, 1)

            def result(b, u, e):
                dve.wait_ge(y_ps, e + 1)
                nc.vector.tensor_copy(yi[:, u:u + 1], meta[:, bass.ds(e, 1), 0:1].rearrange("p a c -> p (a c)"))
                nc.vector.tensor_scalar(ys[:, u, :], ps[:, RESULT[b], 0:D],
                                        meta[:, bass.ds(e, 1), 1:2].rearrange("p a c -> p (a c)"), None,
                                        ALU.mult).then_inc(y_ready, 1)

            gated(0, 0)
            for e in range(NBUF + 1):
                gated((e + 1) % NBUF, e + 1)
                take_hidden(e % 2, e)
                if e >= 1:
                    result((e - 1) % 2, (e - 1) % NBUF, e - 1)

            def later(k, e):
                if not (isinstance(e, int) and e + 1 >= BLK):
                    gated((k + 2) % NBUF, e + 1)
                take_hidden((k + 1) % 2, e)
                dve.wait_ge(y_out[k], (e - (k + 1)) * (16 // NBUF))
                result(k % 2, k, e - 1)

            with dve.Fori(1, E // NBUF - 1) as g:
                for k in range(NBUF):
                    later(k, g * NBUF + (k + 1))
            for k in range(NBUF):
                later(k, E - NBUF + 1 + k)
            dve.wait_ge(y_out[0], 16 * (E // NBUF))
            result(0, 0, E)
            n_over = dve.value_load(ctl[0:1, 0:1], min_val=0, max_val=NOV)
            dve.wait_ge(y_out[1], 16 * (E // NBUF))
            with dve.If(n_over > 1):
                with dve.Fori(1, NOV) as i:
                    with dve.If(i < n_over):
                        gated(0, i + E)
                        take_hidden(0, i + E)
                        result(0, 1, i + E)

            dve.wait_ge(h2_ready, T)
            dve.wait_ge(yb_in[0], 16)
            need(mark(nc.vector.tensor_tensor(acc[:, :, :], h2[:, :, :], yb[:, 0, :, :], ALU.add)))
            dve.wait_ge(yb_in[1], 16)
            nc.vector.tensor_tensor(fin[:, :, :], acc[:, :, :], yb[:, 1, :, :], ALU.add).then_inc(fin_ready, 1)

        @block.tensor
        def _(pe):
            mm = nc.tensor.matmul

            def keep_clock(n, bank=IDLE):
                for _ in range(n):
                    mm(ps[:, bank, 0:P], zeros[:, :], zeros[:, :], start=True, stop=True)

            pe.wait_ge(zeros_set, 1)
            keep_clock(8)
            pe.wait_ge(in_rows, 16)
            pe.wait_ge(ones_set, 1)
            pe.wait_ge(in_first, 16)
            for t in range(T):
                mm(ps[:, t, 0:D], ones[:, :], tokB[:, :], start=True, stop=False)
                for c in range(2):
                    a = (2 * t + c) * B
                    last = mm(ps[:, t, 0:D], xT[:, a:a + P], tokW[:, c, :], start=False, stop=(c == 1))
                last.then_inc(proj_ps, 1)
            keep_clock(24)
            pe.wait_ge(in_table, 16)
            for t in range(T):
                pe.wait_ge(xn_ready, t + 1)
                nc.tensor.transpose(ps[:, t, P:2 * P], xn[:, t, :], ident).then_inc(xnT_ps, 1)

            def values(k):
                return mm(ps[:, VALUES + k // 4, (k % 4) * D:(k % 4 + 1) * D],
                          xnT[:, k, :, :].rearrange("p r b -> p (r b)"),
                          cst[:, C_WQKV + 2 * D:C_WQKV + 3 * D], start=True, stop=True)

            pe.wait_ge(xnT_even, 3)
            pe.wait_ge(xnT_odd, 2)
            for n, part in enumerate((1, 0)):
                w = cst[:, C_WQKV + part * D:C_WQKV + (part + 1) * D]
                mm(ps[:, 2 * n, :], w, xnT[:, 0:8, 0, :], start=True, stop=True)
                mm(ps[:, 2 * n + 1, 0:TOK - 512], w, xnT[:, 8:S, 0, :], start=True, stop=True).then_inc(qk_ps, 1)
            for k in range(S):
                last = values(k)
            last.then_inc(v_ps, 1)

            def scores(i, first=0, end=S):
                o = ps[0:S * H, SCORES[i], P:2 * P]
                if first == 0:
                    if i == 0:
                        pe.wait_ge(bias_ready, 1)
                        pe.wait_ge(k_ready, 1)
                    if i == 2:
                        pe.wait_ge(v_ready, 1)
                    mm(o, bias[:, i, :], cst[0:2, C_PAR:C_PAR + P], start=True, stop=False)
                    if i >= EARLY:
                        pe.wait_ge(prod_ready, i + 1 - EARLY)
                for k in range(first, end):
                    if i < EARLY and k % (S // 2) == 0:
                        pe.wait_ge(prod_first, 2 * i + k // (S // 2) + 1)
                    w = C_HEAD + (S - 1 - k) * H
                    last = mm(o, cst[:, w:w + S * H], prod[:, i, k * P:(k + 1) * P], start=False, stop=(k == S - 1))
                if end == S:
                    last.then_inc(sT_ps, 1)

            def scores_T(i):
                pe.wait_ge(sT_ready, i + 1)
                nc.tensor.transpose(ps[:, SCORES[i], 0:S * H], sT[:, i, :],
                                    cst[0:S * H, C_ID:C_ID + S * H]).then_inc(scores_ps, 1)

            def heads_T(i):
                pe.wait_ge(osum_ready, i + 1)
                nc.tensor.transpose(ps[:, HEADS, 0:P], osum[:, i % 2, :], ident).then_inc(o_ps, 1)

            def stream(i):
                if i == 0:
                    pe.wait_ge(hb_ready, 1)
                pe.wait_ge(sub_ready, i + 1)
                mm(stream_ps(i), ident, hb[:, i, :], start=True, stop=False)

            def project(i):
                pe.wait_ge(oT_ready, i + 1)
                mm(stream_ps(i), oT[:, i, :], outW, start=False, stop=True).then_inc(a_ps, 1)

            def normal_T(i):
                pe.wait_ge(x2_ready, TOPK * i + 1)
                nc.tensor.transpose(ps[:, ROUTE, 0:P], pay[:, 0, i, 0:D], ident).then_inc(x2T_ps, 1)

            def logits(i):
                pe.wait_ge(x2T_ready, i + 1)
                mm(ps[:, ROUTE, P:P + E], x2T[:, i, :], routeW, start=True, stop=True).then_inc(lg_ps, 1)

            def first_rows(i):
                if i >= 1:
                    pe.wait_ge(slot_ready, i)
                pe.wait_ge(x2_ready, TOPK * (i + 1))
                mm(ps[:, SCORES[i], 2 * P:2 * P + E], cst[:, C_ONE:C_ONE + P], filled(i), start=True, stop=False)

            def ranks(i):
                o = ps[:, SCORES[i], 2 * P:2 * P + E]
                pe.wait_ge(mask_ready, i + 1)
                mm(o, cst[:, C_TRI:C_TRI + P], mask[:, i, :], start=False, stop=True).then_inc(rank_ps, 1)

            scores(0)
            scores(1, 0, 1)
            scores_T(0)
            scores(1, 1, S)
            scores(2, 0, 3)
            scores_T(1)
            scores(2, 3, S)
            scores(3, 0, 4)
            scores_T(2)
            for j in range(T + 1):
                if j < T:
                    stream(j)
                if j >= 2:
                    keep_clock(3, FREED)
                if j < T:
                    heads_T(j)
                if j == 0:
                    scores(3, 4, 6)
                if j >= 1:
                    normal_T(j - 1)
                if j == 1:
                    scores(4, 5, 7)
                if j >= 2:
                    keep_clock(1, FREED)
                if j < T:
                    project(j)
                if j >= 1:
                    logits(j - 1)
                if j == 1:
                    scores(4, 7, 8)
                if j == 0:
                    scores(3, 6, S)
                    scores(4, 0, 5)
                    scores_T(3)
                if j == 1:
                    scores(4, 8, S)
                    scores_T(4)
                if j >= 1:
                    first_rows(j - 1)
                    if j >= 2:
                        keep_clock(3, FREED)
                    ranks(j - 1)
            pe.wait_ge(slot_ready, T)
            mm(ps[:, ROUTE, P + 2 * E:P + 3 * E], cst[:, C_ONE:C_ONE + P], filled(T),
               start=True, stop=True).then_inc(cnt_ps, 1)
            keep_clock(16)
            pe.wait_ge(in_expert, 16 * (E // NBUF))

            def rows_T(src, e, landed, count, bank=ROWS_T):
                pe.wait_ge(landed, count)
                nc.tensor.transpose(ps[:, bank, 0:P], xs[:, src, 0:D], ident).then_inc(xsT_ps, 1)

            def gate_up(b, e, w):
                pe.wait_ge(xsT_ready, e + 1)
                mm(ps[:, GATE[b], :], xsT[:, b, :], expW[:, bass.ds(w * WROW, 2 * F)],
                   start=True, stop=True).then_inc(g_ps, 1)

            def hidden_T(b, e):
                pe.wait_ge(hid_ready, e + 2)
                for c in range(2):
                    last = nc.tensor.transpose(ps[:, HID_T, c * P:(c + 1) * P],
                                               hid[:, b, c * P:(c + 1) * P], ident)
                last.then_inc(hidT_ps, 1)

            def down(b, e, w):
                pe.wait_ge(hidT_ready, e + 1)
                for c in range(2):
                    last = mm(ps[:, RESULT[b], 0:D], hidT[:, b, c, :],
                              expW[:, bass.ds(w * WROW + (2 * F + c * D), D)], start=(c == 0), stop=(c == 1))
                last.then_inc(y_ps, 1)

            def step(r, e):
                in_loop = not isinstance(e, int)
                n = r + 3
                if in_loop or e + 3 < BLK:
                    pe.wait_ge(xsT_ready, e + 3)
                    rows_T(n % NBUF, e + 3, xs_in[n % NBUF], (e - r) * (16 // NBUF) + 16 * (n // NBUF + 1))
                if in_loop or e + 2 < BLK:
                    if in_loop or e >= 1:
                        pe.wait_ge(hid_ready, e)
                    gate_up((r + 2) % NBUF, e + 2, e + 2 if in_loop or e + 2 < E else owner0)
                if in_loop or e >= 1:
                    pe.wait_ge(hidT_ready, e)
                hidden_T(r % 2, e)
                if in_loop or e >= 1:
                    down((r + 1) % 2, e - 1, e - 1)

            rows_T(0, 0, xs_in[0], 16, FIRST_ROWS[0])
            rows_T(1, 1, xs_in[1], 16, FIRST_ROWS[1])
            gate_up(0, 0, 0)
            rows_T(2, 2, xs_in[2], 16, FIRST_ROWS[2])
            gate_up(1, 1, 1)
            step(0, 0)
            with pe.Fori(0, E // NBUF - 1) as g:
                for k in range(NBUF):
                    step(k + 1, g * NBUF + (k + 1))
            step((E - 3) % NBUF, E - 3)
            pe.wait_ge(ctl_ready, 1)
            n_over = pe.value_load(ctl[0:1, 0:1], min_val=0, max_val=NOV)
            owner0 = pe.value_load(ctl[0:1, 1:2], min_val=0, max_val=E - 1)
            for e in range(E - 2, BLK):
                step(e % NBUF, e)
            down(0, E, owner0)
            with pe.If(n_over > 1):
                with pe.Fori(1, NOV) as i:
                    with pe.If(i < n_over):
                        owner = pe.value_load(ctl[0:1, bass.ds(i + 1, 1)], min_val=0, max_val=E - 1)
                        rows_T(0, i + E, xs_over, i * 16)
                        gate_up(0, i + E, owner)
                        hidden_T(0, i + E)
                        down(0, i + E, owner)


_ARGS = ["first", "rows", "gb", "t_head", "table", "expert_w"]



def kernel(x, L0_tok_W, L0_tok_b, L0_tok_gamma, L0_tok_beta, L0_attn_in_proj_w, L0_attn_in_proj_b,
           L0_attn_out_proj_w, L0_attn_out_proj_b, L0_attn_t, L0_ffn_router_w, L0_ffn_gate_w,
           L0_ffn_up_w, L0_ffn_down_w):
    import numpy as _np
    import concourse.bacc as _bacc
    from concourse import mybir as _mybir
    from concourse.bass_utils import run_bass_kernel_spmd as _run

    a = _np.ascontiguousarray
    xf = _np.asarray(x).reshape(B, -1)[:, :CHUNKS * P]
    ex = [a(_np.asarray(L0_ffn_gate_w).transpose(1, 0, 2)),
          a(_np.asarray(L0_ffn_up_w).transpose(1, 0, 2)),
          a(_np.asarray(L0_ffn_down_w).reshape(E, 2, P, D).transpose(2, 0, 1, 3).reshape(P, E, 2 * D))]
    inb = _np.asarray(L0_attn_in_proj_b)
    x_t = xf.reshape(B, CHUNKS, P).transpose(2, 1, 0).reshape(P, CHUNKS * B)
    tok_w = _np.asarray(L0_tok_W).reshape(2, P, D).transpose(1, 0, 2).reshape(P, 2 * D)
    data = {
        "first": _np.concatenate([x_t, tok_w], axis=1),
        "rows": _np.asarray(L0_tok_b).reshape(1, D),
        "gb": _np.concatenate([_np.asarray(v) for v in (L0_tok_gamma, L0_tok_beta, L0_attn_out_proj_b)]),
        "t_head": _np.asarray(L0_attn_t),
        "table": _np.concatenate([constants(), _np.asarray(L0_attn_in_proj_w).T, _np.asarray(L0_attn_out_proj_w).T,
                                  _np.asarray(L0_ffn_router_w).T, inb.reshape(3, D).T], axis=1),
        "expert_w": _np.concatenate(ex, axis=2).reshape(P, E * WROW),
    }
    nc = _bacc.Bacc("TRN2", target_bir_lowering=False, num_devices=1)
    arrays, args = {}, []
    for name in _ARGS:
        v = a(data[name])
        arrays[name + "_dram"] = v
        args.append(nc.dram_tensor(name + "_dram", v.shape, _mybir.dt.from_np(v.dtype), kind="ExternalInput").ap())
    out = nc.dram_tensor("out_dram", (B, S, D), _mybir.dt.float32, kind="ExternalOutput").ap()
    audio_tower(nc, *args, out)
    r = _run(nc, [arrays], core_ids=[0])
    return r.results[0]["out_dram"]
```
